# Optimizing a Trainium2 kernel written in Bass

```python
import numpy as np
import jax
import jax.numpy as jnp

def _softmax(x, axis=-1):
    return jax.nn.softmax(x, axis=axis)

def _gelu(x):
    return jax.nn.gelu(x, approximate=True)

def _silu(x):
    return jax.nn.silu(x)

def _sigmoid(x):
    return jax.nn.sigmoid(x)

def _layernorm(x, axis=-1, eps=1e-05):
    m = jnp.mean(x, axis=axis, keepdims=True)
    v = jnp.var(x, axis=axis, keepdims=True)
    return (x - m) / jnp.sqrt(v + eps)

def _scatter_add(tgt, idx, src, axis=0):
    return tgt.at[idx].add(src)

def _segment_sum(src, seg, n):
    return jax.ops.segment_sum(src, seg, n)
kernel_name = 'mk_conv_seq_d2_conv_nchw256_r2_7018dc'

def setup_inputs(seed: int=0):
    np.random.seed(seed)
    _w = jnp.asarray

    def _rec_inputs():
        import jax
        import jax.numpy as jnp
        _gk = jax.random.key(seed)
        x = -0.0002928 + 1 * jax.random.normal(jax.random.fold_in(_gk, 1), (4, 128, 32, 32), jnp.float32)
        return x
    x = _rec_inputs()

    def _L0_conv_setup():
        import jax, jax.numpy as jnp
        import numpy as np
        D_MODEL = 128
        EXPAND = 2
        D_STATE = 16
        D_CONV = 4
        D_INNER = EXPAND * D_MODEL
        DT_RANK = (D_MODEL + 15) // 16

        def _mamba_params(key):
            ks = jax.random.split(key, 5)

            def rn(k, shape, scale):
                return jax.random.normal(k, shape, jnp.float32) * scale
            return dict(W_in=rn(ks[0], (2 * D_INNER, D_MODEL), D_MODEL ** (-0.5)), conv_w=rn(ks[1], (D_INNER, D_CONV), D_CONV ** (-0.5)), conv_b=jnp.zeros((D_INNER,), jnp.float32), W_x=rn(ks[2], (DT_RANK + 2 * D_STATE, D_INNER), D_INNER ** (-0.5)), W_dt=rn(ks[3], (D_INNER, DT_RANK), DT_RANK ** (-0.5)), b_dt=jnp.full((D_INNER,), -4.0, jnp.float32), A_log=jnp.log(jnp.broadcast_to(jnp.arange(1, D_STATE + 1, dtype=jnp.float32), (D_INNER, D_STATE))), D_skip=jnp.ones((D_INNER,), jnp.float32), W_out=rn(ks[4], (D_MODEL, D_INNER), D_INNER ** (-0.5)))

        def _mamba(x, W_in, conv_w, conv_b, W_x, W_dt, b_dt, A_log, D_skip, W_out):
            B, L, _ = x.shape
            xz = jnp.einsum('bld,ed->ble', x, W_in)
            xc, z = jnp.split(xz, 2, axis=-1)
            xt = jnp.transpose(xc, (0, 2, 1))
            xt = jax.lax.conv_general_dilated(xt, conv_w[:, None, :], (1,), [(D_CONV - 1, 0)], feature_group_count=D_INNER)
            xc = jax.nn.silu(jnp.transpose(xt, (0, 2, 1)) + conv_b)
            dbc = jnp.einsum('ble,re->blr', xc, W_x)
            dt = jax.nn.softplus(jnp.einsum('blr,er->ble', dbc[..., :DT_RANK], W_dt) + b_dt)
            Bm = dbc[..., DT_RANK:DT_RANK + D_STATE]
            Cm = dbc[..., DT_RANK + D_STATE:]
            A = -jnp.exp(A_log)

            def step(h, inp):
                dt_t, B_t, C_t, x_t = inp
                dA = jnp.exp(dt_t[:, :, None] * A)
                h = dA * h + (dt_t * x_t)[:, :, None] * B_t[:, None, :]
                return (h, jnp.einsum('bdn,bn->bd', h, C_t))
            h0 = jnp.zeros((B, D_INNER, D_STATE), x.dtype)
            xs = (jnp.transpose(dt, (1, 0, 2)), jnp.transpose(Bm, (1, 0, 2)), jnp.transpose(Cm, (1, 0, 2)), jnp.transpose(xc, (1, 0, 2)))
            _, ys = jax.lax.scan(step, h0, xs)
            y = jnp.transpose(ys, (1, 0, 2)) + xc * D_skip
            y = y * jax.nn.silu(z)
            return jnp.einsum('ble,de->bld', y, W_out)
        key = jax.random.key(seed)
        kx, k1, k2 = jax.random.split(key, 3)
        x = jax.random.normal(kx, (4, D_MODEL, 32, 32), jnp.float32)
        p1 = {k + '1': v for k, v in _mamba_params(k1).items()}
        p2 = {k + '2': v for k, v in _mamba_params(k2).items()}
        return {'x': x, **p1, **p2}
    _L0_conv_all = _L0_conv_setup()
    _L0_conv_in = {k: v for k, v in _L0_conv_all.items() if k in ('W_in1', 'conv_w1', 'conv_b1', 'W_x1', 'W_dt1', 'b_dt1', 'A_log1', 'D_skip1', 'W_out1', 'W_in2', 'conv_w2', 'conv_b2', 'W_x2', 'W_dt2', 'b_dt2', 'A_log2', 'D_skip2', 'W_out2')}
    del _L0_conv_all

    def _L1_conv_setup():
        import jax, jax.numpy as jnp
        import numpy as np
        EPS = 1e-05

        def batch_norm(x, gamma, beta):
            mean = jnp.mean(x, axis=(0, 2, 3), keepdims=True)
            var = jnp.mean((x - mean) ** 2, axis=(0, 2, 3), keepdims=True)
            xhat = (x - mean) * jax.lax.rsqrt(var + EPS)
            return xhat * gamma[None, :, None, None] + beta[None, :, None, None]

        def quantize_w1bit(w):
            E = jax.lax.stop_gradient(jnp.mean(jnp.abs(w)))
            wq = E * jnp.sign(w)
            return w + jax.lax.stop_gradient(wq - w)

        def conv3x3(x, w):
            return jax.lax.conv_general_dilated(x, w, window_strides=(1, 1), padding=((1, 1), (1, 1)), dimension_numbers=('NCHW', 'OIHW', 'NCHW'))
        key = jax.random.key(seed)
        ks = jax.random.split(key, 3)
        B, Cin, Cout, H, W = (32, 128, 128, 56, 56)
        return {'x': jax.random.normal(ks[0], (B, Cin, H, W), jnp.float32), 'gamma0': jnp.ones((Cin,), jnp.float32), 'beta0': jnp.zeros((Cin,), jnp.float32), 'w0': jax.random.normal(ks[1], (Cout, Cin, 3, 3), jnp.float32) * 0.05, 'gamma1': jnp.ones((Cout,), jnp.float32), 'beta1': jnp.zeros((Cout,), jnp.float32), 'w1': jax.random.normal(ks[2], (Cout, Cout, 3, 3), jnp.float32) * 0.05}
    _L1_conv_all = _L1_conv_setup()
    _L1_conv_in = {k: v for k, v in _L1_conv_all.items() if k in ('gamma0', 'beta0', 'w0', 'gamma1', 'beta1', 'w1')}
    del _L1_conv_all
    return {'x': x, 'L0_conv_W_in1': _L0_conv_in['W_in1'], 'L0_conv_conv_w1': _L0_conv_in['conv_w1'], 'L0_conv_conv_b1': _L0_conv_in['conv_b1'], 'L0_conv_W_x1': _L0_conv_in['W_x1'], 'L0_conv_W_dt1': _L0_conv_in['W_dt1'], 'L0_conv_b_dt1': _L0_conv_in['b_dt1'], 'L0_conv_A_log1': _L0_conv_in['A_log1'], 'L0_conv_D_skip1': _L0_conv_in['D_skip1'], 'L0_conv_W_out1': _L0_conv_in['W_out1'], 'L0_conv_W_in2': _L0_conv_in['W_in2'], 'L0_conv_conv_w2': _L0_conv_in['conv_w2'], 'L0_conv_conv_b2': _L0_conv_in['conv_b2'], 'L0_conv_W_x2': _L0_conv_in['W_x2'], 'L0_conv_W_dt2': _L0_conv_in['W_dt2'], 'L0_conv_b_dt2': _L0_conv_in['b_dt2'], 'L0_conv_A_log2': _L0_conv_in['A_log2'], 'L0_conv_D_skip2': _L0_conv_in['D_skip2'], 'L0_conv_W_out2': _L0_conv_in['W_out2'], 'L1_conv_gamma0': _L1_conv_in['gamma0'], 'L1_conv_beta0': _L1_conv_in['beta0'], 'L1_conv_w0': _L1_conv_in['w0'], 'L1_conv_gamma1': _L1_conv_in['gamma1'], 'L1_conv_beta1': _L1_conv_in['beta1'], 'L1_conv_w1': _L1_conv_in['w1']}

def reference(x, L0_conv_W_in1, L0_conv_conv_w1, L0_conv_conv_b1, L0_conv_W_x1, L0_conv_W_dt1, L0_conv_b_dt1, L0_conv_A_log1, L0_conv_D_skip1, L0_conv_W_out1, L0_conv_W_in2, L0_conv_conv_w2, L0_conv_conv_b2, L0_conv_W_x2, L0_conv_W_dt2, L0_conv_b_dt2, L0_conv_A_log2, L0_conv_D_skip2, L0_conv_W_out2, L1_conv_gamma0, L1_conv_beta0, L1_conv_w0, L1_conv_gamma1, L1_conv_beta1, L1_conv_w1):
    import jax
    import jax.numpy as jnp

    def _L0_conv_ref(x, W_in1, conv_w1, conv_b1, W_x1, W_dt1, b_dt1, A_log1, D_skip1, W_out1, W_in2, conv_w2, conv_b2, W_x2, W_dt2, b_dt2, A_log2, D_skip2, W_out2):
        import jax, jax.numpy as jnp
        import numpy as np
        D_MODEL = 128
        EXPAND = 2
        D_STATE = 16
        D_CONV = 4
        D_INNER = EXPAND * D_MODEL
        DT_RANK = (D_MODEL + 15) // 16

        def _mamba_params(key):
            ks = jax.random.split(key, 5)

            def rn(k, shape, scale):
                return jax.random.normal(k, shape, jnp.float32) * scale
            return dict(W_in=rn(ks[0], (2 * D_INNER, D_MODEL), D_MODEL ** (-0.5)), conv_w=rn(ks[1], (D_INNER, D_CONV), D_CONV ** (-0.5)), conv_b=jnp.zeros((D_INNER,), jnp.float32), W_x=rn(ks[2], (DT_RANK + 2 * D_STATE, D_INNER), D_INNER ** (-0.5)), W_dt=rn(ks[3], (D_INNER, DT_RANK), DT_RANK ** (-0.5)), b_dt=jnp.full((D_INNER,), -4.0, jnp.float32), A_log=jnp.log(jnp.broadcast_to(jnp.arange(1, D_STATE + 1, dtype=jnp.float32), (D_INNER, D_STATE))), D_skip=jnp.ones((D_INNER,), jnp.float32), W_out=rn(ks[4], (D_MODEL, D_INNER), D_INNER ** (-0.5)))

        def _mamba(x, W_in, conv_w, conv_b, W_x, W_dt, b_dt, A_log, D_skip, W_out):
            B, L, _ = x.shape
            xz = jnp.einsum('bld,ed->ble', x, W_in)
            xc, z = jnp.split(xz, 2, axis=-1)
            xt = jnp.transpose(xc, (0, 2, 1))
            xt = jax.lax.conv_general_dilated(xt, conv_w[:, None, :], (1,), [(D_CONV - 1, 0)], feature_group_count=D_INNER)
            xc = jax.nn.silu(jnp.transpose(xt, (0, 2, 1)) + conv_b)
            dbc = jnp.einsum('ble,re->blr', xc, W_x)
            dt = jax.nn.softplus(jnp.einsum('blr,er->ble', dbc[..., :DT_RANK], W_dt) + b_dt)
            Bm = dbc[..., DT_RANK:DT_RANK + D_STATE]
            Cm = dbc[..., DT_RANK + D_STATE:]
            A = -jnp.exp(A_log)

            def step(h, inp):
                dt_t, B_t, C_t, x_t = inp
                dA = jnp.exp(dt_t[:, :, None] * A)
                h = dA * h + (dt_t * x_t)[:, :, None] * B_t[:, None, :]
                return (h, jnp.einsum('bdn,bn->bd', h, C_t))
            h0 = jnp.zeros((B, D_INNER, D_STATE), x.dtype)
            xs = (jnp.transpose(dt, (1, 0, 2)), jnp.transpose(Bm, (1, 0, 2)), jnp.transpose(Cm, (1, 0, 2)), jnp.transpose(xc, (1, 0, 2)))
            _, ys = jax.lax.scan(step, h0, xs)
            y = jnp.transpose(ys, (1, 0, 2)) + xc * D_skip
            y = y * jax.nn.silu(z)
            return jnp.einsum('ble,de->bld', y, W_out)
        b, c, h, w = x.shape
        x1 = x.reshape(b * h, w, c)
        x2 = x.reshape(b * w, h, c)
        y1 = _mamba(x1, W_in1, conv_w1, conv_b1, W_x1, W_dt1, b_dt1, A_log1, D_skip1, W_out1).reshape(b, c, h, w)
        y2 = _mamba(x2, W_in2, conv_w2, conv_b2, W_x2, W_dt2, b_dt2, A_log2, D_skip2, W_out2).reshape(b, c, h, w)
        return y1 + y2 + x

    def _L1_conv_ref(x, gamma0, beta0, w0, gamma1, beta1, w1):
        import jax, jax.numpy as jnp
        import numpy as np
        EPS = 1e-05

        def batch_norm(x, gamma, beta):
            mean = jnp.mean(x, axis=(0, 2, 3), keepdims=True)
            var = jnp.mean((x - mean) ** 2, axis=(0, 2, 3), keepdims=True)
            xhat = (x - mean) * jax.lax.rsqrt(var + EPS)
            return xhat * gamma[None, :, None, None] + beta[None, :, None, None]

        def quantize_w1bit(w):
            E = jax.lax.stop_gradient(jnp.mean(jnp.abs(w)))
            wq = E * jnp.sign(w)
            return w + jax.lax.stop_gradient(wq - w)

        def conv3x3(x, w):
            return jax.lax.conv_general_dilated(x, w, window_strides=(1, 1), padding=((1, 1), (1, 1)), dimension_numbers=('NCHW', 'OIHW', 'NCHW'))
        out = jax.nn.relu(batch_norm(x, gamma0, beta0))
        shortcut = x
        out = conv3x3(out, quantize_w1bit(w0))
        out = jax.nn.relu(batch_norm(out, gamma1, beta1))
        out = conv3x3(out, quantize_w1bit(w1))
        return out + shortcut

    def _gn(v, G=32, eps=1e-05):
        B_, C_, H_, W_ = v.shape
        g = v.reshape(B_, G, C_ // G, H_, W_)
        m = jnp.mean(g, axis=(2, 3, 4), keepdims=True)
        s = jnp.var(g, axis=(2, 3, 4), keepdims=True)
        return ((g - m) / jnp.sqrt(s + eps)).reshape(v.shape)

    def _ln_c(v, eps=1e-06):
        m = jnp.mean(v, axis=1, keepdims=True)
        s = jnp.var(v, axis=1, keepdims=True)
        return (v - m) / jnp.sqrt(s + eps)

    def _ln_t(v, eps=1e-05):
        m = jnp.mean(v, axis=-1, keepdims=True)
        s = jnp.var(v, axis=-1, keepdims=True)
        return (v - m) / jnp.sqrt(s + eps)

    def _to_tokens(v):
        B_, C_, H_, W_ = v.shape
        return v.reshape(B_, C_, H_ * W_).transpose(0, 2, 1)

    def _from_tokens(t, like):
        B_, C_, H_, W_ = like.shape
        return t.transpose(0, 2, 1).reshape(B_, C_, H_, W_)
    x = _L0_conv_ref(x, L0_conv_W_in1, L0_conv_conv_w1, L0_conv_conv_b1, L0_conv_W_x1, L0_conv_W_dt1, L0_conv_b_dt1, L0_conv_A_log1, L0_conv_D_skip1, L0_conv_W_out1, L0_conv_W_in2, L0_conv_conv_w2, L0_conv_conv_b2, L0_conv_W_x2, L0_conv_W_dt2, L0_conv_b_dt2, L0_conv_A_log2, L0_conv_D_skip2, L0_conv_W_out2)
    x = _L1_conv_ref(x, L1_conv_gamma0, L1_conv_beta0, L1_conv_w0, L1_conv_gamma1, L1_conv_beta1, L1_conv_w1)
    return x

_drawn_inputs = setup_inputs


def setup_inputs(seed=0):
    import zlib

    import numpy as np

    out = dict(_drawn_inputs(seed))
    spreads = {'L0_conv_conv_b1': (0.0, 0.1),
     'L0_conv_b_dt1': (-4.0, 0.6),
     'L0_conv_D_skip1': (1.0, 0.2),
     'L0_conv_conv_b2': (0.0, 0.1),
     'L0_conv_b_dt2': (-4.0, 0.6),
     'L0_conv_D_skip2': (1.0, 0.2),
     'L1_conv_gamma0': (1.0, 0.2),
     'L1_conv_beta0': (0.0, 0.1),
     'L1_conv_gamma1': (1.0, 0.2),
     'L1_conv_beta1': (0.0, 0.1)}
    factors = {'L0_conv_A_log1': 3.239}
    for name, (base, spread) in spreads.items():
        noise = np.random.default_rng([zlib.crc32(name.encode()), seed]).standard_normal(out[name].shape)
        drawn = base * np.exp(spread * noise) if base else spread * noise
        out[name] = jnp.asarray(drawn.astype(out[name].dtype))
    for name, factor in factors.items():
        out[name] = (out[name] * factor).astype(out[name].dtype)
    return out
```

```python
from contextlib import ExitStack

import concourse.bass as bass
from concourse import mybir

ALU = mybir.AluOpType
ACT = mybir.ActivationFunctionType
AX = mybir.AxisListType
F32 = mybir.dt.float32
BF16 = mybir.dt.bfloat16

NB, C, H, W = 4, 128, 32, 32
HW = H * W
D = C
L = W
E_IN = 2 * D
HALVES = E_IN // 128
NST = 16
RANK = D // 16
VECTORS = 3
KCONV = 4
TOKENS = NB * HW
CHUNK = 512
CSEQ = CHUNK // L
MAMBAS = 2
CHUNKS_PER_IMAGE = HW // CHUNK
ITEMS_PER_IMAGE = CHUNKS_PER_IMAGE * MAMBAS
ITEMS = NB * ITEMS_PER_IMAGE
BC = 2 * NST
PARTS = 3
LPAD = KCONV - 1
TAPS = 9
EPS = 1e-5
HP, WP = H + 2, W + 2
TILES = NB * 2
ROWS = H // 2
WCOUNT = C * C * TAPS

SLOTS = 8
LAG = 3
COPIES = 3

POOL_B = (0, 2, 3, 5, 7, 8, 10, 12, 15)
POOL_C = (1, 3, 4, 6, 8, 9, 11, 12, 14)

AT_PROJ, AT_CONV, AT_SILU, AT_DBC, AT_SPLIT, AT_DT = 0, 1, 5, 6, 7, 7
AT_EXP, AT_LN, AT_RES, AT_SUM = 9, 10, 11, 12
AT_POST = LAG
AT_OUT = NST - 8


def mamba_conv_kernel(nc, t, out):
    x = t["x"]
    ctx = ExitStack()
    with ctx:
        def sb(name, shape, dt=F32):
            return ctx.enter_context(nc.sbuf_tensor(name, shape, dt))

        def sem(name):
            return ctx.enter_context(nc.semaphore(name))

        ident = sb("ident", [128, 128])
        ident16 = sb("ident16", [128, 128], BF16)
        ones = sb("ones", [128, 128])
        sel = sb("sel", [PARTS * 32, BC, 128], BF16)
        eps = sb("eps", [128, 1])
        state = sb("state", [128, SLOTS, HALVES, CHUNK])
        raw = state[:, :, :, :].rearrange("p a h n -> p (a h n)")
        raw_used = [0]

        def staged(columns):
            raw_used[0] += columns
            assert raw_used[0] <= SLOTS * HALVES * CHUNK
            return raw[:, raw_used[0] - columns:raw_used[0]]

        XROWS = PARTS * 32 + RANK
        w_in_raw = [staged(4 * 128).rearrange("p (a d) -> p a d", a=4) for m in range(2)]
        w_x_raw = [staged(E_IN)[0:XROWS, :] for m in range(2)]
        w_dt_raw = [staged(HALVES * XROWS).rearrange("p (a r) -> p a r", a=HALVES) for m in range(2)]
        w_out_raw = [staged(E_IN) for m in range(2)]
        vectors_raw = [staged(128)[0:VECTORS * HALVES, :] for m in range(2)]
        k_raw = [staged(C * TAPS) for n in range(2)]
        k_sign = [staged(C * TAPS // 2).bitcast(BF16) for n in range(2)]
        w_in = [sb(f"w_in{m}", [128, 4, 128]) for m in range(2)]
        w_x = [sb(f"w_x{m}", [128, HALVES, PARTS * 32 + RANK]) for m in range(2)]
        w_dt = [sb(f"w_dt{m}", [PARTS * 32 + RANK, E_IN]) for m in range(2)]
        w_out = [sb(f"w_out{m}", [128, HALVES, 128]) for m in range(2)]
        conv_w = [sb(f"conv_w{m}", [128, HALVES, KCONV]) for m in range(2)]
        vectors = [sb(f"vectors{m}", [128, VECTORS * HALVES]) for m in range(2)]
        conv_b, b_dt, d_skip = ([vectors[m][:, HALVES * v:HALVES * v + HALVES] for m in range(2)]
                                for v in range(VECTORS))
        a_neg = [sb(f"a_neg{m}", [128, HALVES, NST]) for m in range(2)]
        k_t = [sb(f"k_t{n}", [128, TAPS, 128], BF16) for n in range(2)]
        k_abs = sb("k_abs", [128, 2])
        k_mean = sb("k_mean", [128, 2])
        k_mean_sq = sb("k_mean_sq", [128, 2])
        gamma = [sb(f"gamma{n}", [128, 1]) for n in range(2)]
        beta = [sb(f"beta{n}", [128, 1]) for n in range(2)]

        x_tok = sb("x_tok", [128, TOKENS // 128, 128])
        y_gated = x_tok[:, :, :].rearrange("p a d -> p (a d)").rearrange("p (g n) -> p g n", g=4)
        x_t = sb("x_t", [128, TOKENS])
        res = sb("res", [128, NB, HW])
        xpad = sb("xpad", [128, HALVES, CSEQ, LPAD + L])
        cv = sb("cv", [128, HALVES, CHUNK])
        xc = [sb(f"xc{m}", [128, HALVES, CHUNK]) for m in range(2)]
        gate = [sb(f"gate{m}", [128, HALVES, CHUNK]) for m in range(2)]
        dt = [sb(f"dt{m}", [128, HALVES, CHUNK]) for m in range(2)]
        u = [sb(f"u{m}", [128, HALVES, CHUNK]) for m in range(2)]
        split = [sb(f"split{m}", [PARTS * 32, CHUNK], BF16) for m in range(2)]
        split_rest = sb("split_rest", [64, CHUNK])
        dt_low = sb("dt_low", [PARTS * 32 + RANK, CHUNK])
        sp_e = sb("sp_e", [128, HALVES, CHUNK])
        sp_relu = sb("sp_relu", [128, HALVES, CHUNK])
        sp_ln = sb("sp_ln", [128, HALVES, CHUNK])
        sp_one = sb("sp_one", [128, HALVES, CHUNK])
        b_copy = sb("b_copy", [128, COPIES, CHUNK])
        c_copy = sb("c_copy", [128, COPIES, CHUNK])
        pad = [sb(f"pad{p}", [128, NB, HP, WP], BF16) for p in range(PARTS)]
        act_f, act_r = b_copy[:, 0:2, :], c_copy[:, 0:2, :]
        stats = sb("stats", [128, TILES, 6])
        mv = sb("mv", [128, 2])
        bn_tmp = sb("bn_tmp", [128, 4])
        bn_a = [sb(f"bn_a{n}", [128, 1]) for n in range(2)]
        bn_b = [sb(f"bn_b{n}", [128, 1]) for n in range(2)]

        bank = [ctx.enter_context(nc.psum_tensor(f"bank{i}", [128, CHUNK], F32)) for i in range(8)]
        decay = bank[0:2]
        b_row, c_row = bank[2], bank[3]
        y_sum = bank[4:6]
        work = bank[6:8]

        load_w = sem("load_w")
        load_x = sem("load_x")
        load_res = sem("load_res")
        load_k = sem("load_k")
        consts = sem("consts")
        zeros = sem("zeros")
        pads_zero = sem("pads_zero")
        identities = sem("identities")
        a_exp = sem("a_exp")
        a_ready = sem("a_ready")
        k_signed = sem("k_signed")
        k_summed = sem("k_summed")
        k_mean_mm = sem("k_mean_mm")
        k_mean_ready = sem("k_mean_ready")
        setup_mm = sem("setup_mm")
        setup_act = sem("setup_act")
        setup_dve = sem("setup_dve")
        pre_mm = sem("pre_mm")
        xpad_ready = sem("xpad_ready")
        tap_done = sem("tap_done")
        xc_ready = sem("xc_ready")
        gate_ready = sem("gate_ready")
        dt_low_ready = sem("dt_low_ready")
        hi_ready = sem("hi_ready")
        rest_ready = sem("rest_ready")
        mid_ready = sem("mid_ready")
        split_ready = sem("split_ready")
        abs_ready = sem("abs_ready")
        relu_ready = sem("relu_ready")
        exp_ready = sem("exp_ready")
        ln_ready = sem("ln_ready")
        one_ready = sem("one_ready")
        lost_ready = sem("lost_ready")
        log1p_ready = sem("log1p_ready")
        dt_ready = sem("dt_ready")
        u_ready = sem("u_ready")
        b_ready = sem("b_ready")
        c_ready = sem("c_ready")
        b_copied = sem("b_copied")
        c_copied = sem("c_copied")
        decay_ready = sem("decay_ready")
        input_dve = sem("input_dve")
        input_pool = sem("input_pool")
        scanned = sem("scanned")
        output_dve = sem("output_dve")
        output_pool = sem("output_pool")
        summed = sem("summed")
        y_read = sem("y_read")
        gated = sem("gated")
        out_mm = sem("out_mm")
        res_added = sem("res_added")
        stat_done = sem("stat_done")
        bn_mv = sem("bn_mv")
        bn_std = sem("bn_std")
        bn_step = sem("bn_step")
        bn_ready = sem("bn_ready")
        act_hi = sem("act_hi")
        act_full = sem("act_full")
        act_rest = sem("act_rest")
        act_mid = sem("act_mid")
        act_lo = sem("act_lo")
        conv_mm = sem("conv_mm")
        y_ready = sem("y_ready")
        y_stored = sem("y_stored")

        block = ctx.enter_context(nc.Block())

        def wait(eng, semaphore, count, per_item, i):
            if count > 0:
                eng.wait_ge(semaphore, count + i * (per_item * ITEMS_PER_IMAGE))

        def wait_image(eng, semaphore, count, i):
            if count > 0:
                eng.wait_ge(semaphore, count + i * 2)

        def taken(states, n):
            return n // NST * len(states) + sum(s < n % NST for s in states)

        def run_items(eng, slot):
            for s in range(NST):
                slot(0, s, 0)
            with eng.Fori(0, NB - 1) as i:
                for k in range(1, ITEMS_PER_IMAGE + 1):
                    for s in range(NST):
                        slot(k, s, i)
            for k in range(ITEMS - ITEMS_PER_IMAGE + 1, ITEMS):
                for s in range(NST):
                    slot(k, s, 0)

        LAST = ITEMS * NST

        def wait_input(eng, n, i):
            if n % NST in POOL_B:
                wait(eng, input_pool, taken(POOL_B, n) + 1, len(POOL_B), i)
            else:
                wait(eng, input_dve, n - taken(POOL_B, n) + 1, NST - len(POOL_B), i)

        def wait_output(eng, n, i):
            if n % NST in POOL_C:
                wait(eng, output_pool, taken(POOL_C, n) + 1, len(POOL_C), i)
            else:
                wait(eng, output_dve, n - taken(POOL_C, n) + 1, NST - len(POOL_C), i)

        def b_slot(n):
            return sum(s < n % NST for s in POOL_B) % COPIES

        def c_slot(n):
            return sum(s < n % NST for s in POOL_C) % COPIES

        def earlier(states, n):
            j = sum(s < n % NST for s in states)
            total = n // NST * len(states)
            if j >= COPIES:
                return total + j - COPIES + 1
            last = max(q for q in range(len(states)) if q % COPIES == j % COPIES)
            return total - len(states) + last + 1

        def inner(part, n):
            b, r = n // 2, ROWS * (n % 2)
            return pad[part][:, b, 1 + r:1 + r + ROWS, 1:1 + W]

        def tile(n):
            return state[:, n % SLOTS, :, :]

        def over_halves(row):
            return row.unsqueeze(1).to_broadcast([128, HALVES, CHUNK])

        SETUP_BANKS = (4, 5, 6, 7)

        @block.sync
        def _(sp):
            for m in range(2):
                s = str(m + 1)
                sp.dma_start(w_in_raw[m][:, :, :],
                             t[f"L0_conv_W_in{s}"].rearrange("(a p) d -> p a d", p=128)).then_inc(load_w, 16)
                if m == 0:
                    rows = x.rearrange("b c h w -> (b c h w)").rearrange("(a p d) -> p a d", p=128, d=D)
                    for q in range(4):
                        n = TOKENS // 128 // 4
                        sp.dma_start(x_tok[:, q * n:(q + 1) * n, :],
                                     rows[:, q * n:(q + 1) * n, :]).then_inc(load_x, 16)
                w = t[f"L0_conv_W_x{s}"]
                for part in range(PARTS):
                    sp.dma_start(w_x_raw[m][32 * part:32 * part + 32, :], w[RANK:RANK + BC, :]).then_inc(load_w, 16)
                sp.dma_start(w_x_raw[m][PARTS * 32:PARTS * 32 + RANK, :], w[0:RANK, :]).then_inc(load_w, 16)
                sp.dma_start(w_out_raw[m][:, :], t[f"L0_conv_W_out{s}"]).then_inc(load_w, 16)
                sp.wait_ge(zeros, 2)
                sp.dma_start(w_dt_raw[m][:, :, PARTS * 32:],
                             t[f"L0_conv_W_dt{s}"].rearrange("(a p) r -> p a r", p=128)).then_inc(load_w, 16)
                sp.dma_start(conv_w[m][:, :, :],
                             t[f"L0_conv_conv_w{s}"].rearrange("(a p) k -> p a k", p=128)).then_inc(load_w, 16)
                sp.dma_start(a_neg[m][:, :, :],
                             t[f"L0_conv_A_log{s}"].rearrange("(a p) n -> p a n", p=128)).then_inc(load_w, 16)
                for v, name in enumerate(("conv_b", "b_dt", "D_skip")):
                    sp.dma_start(vectors_raw[m][HALVES * v:HALVES * v + HALVES, :],
                                 t[f"L0_conv_{name}{s}"].rearrange("(a p) -> a p", p=128)).then_inc(load_w, 16)
            for n in range(2):
                sp.dma_start(k_raw[n][:, :], t[f"L1_conv_w{n}"].rearrange("o i a b -> o (i a b)")).then_inc(load_k, 16)
                sp.dma_start(gamma[n][:, :], t[f"L1_conv_gamma{n}"].rearrange("(p a) -> p a", a=1)).then_inc(load_k, 16)
                sp.dma_start(beta[n][:, :], t[f"L1_conv_beta{n}"].rearrange("(p a) -> p a", a=1)).then_inc(load_k, 16)
            for b in range(NB):
                sp.dma_start(res[:, b, :], x[b].rearrange("c h w -> c (h w)")).then_inc(load_res, 16)
            for n in range(TILES):
                sp.wait_ge(y_ready, n + 1)
                b, half = n // 2, n % 2
                sp.dma_start(out[b].rearrange("c h w -> c (h w)")[:, half * CHUNK:(half + 1) * CHUNK],
                             res[:, b, half * CHUNK:(half + 1) * CHUNK]).then_inc(y_stored, 16)
            sp.wait_ge(y_stored, 16 * TILES)

        W_LOADS = 16 * MAMBAS * (1 + PARTS + 1 + 1 + 1 + 1 + 1 + 3)
        K_LOADS = 16 * 2 * 3

        def setup_groups():
            for m in range(2):
                yield ("w", [(w_in_raw[m][:, a, :], 128, 128 * a) for a in range(4)],
                       w_in[m][:, :, :].rearrange("p a e -> p (a e)"), 128, 0, 512)
                yield ("w", [(w_x_raw[m][:, 128 * h:128 * h + 128], PARTS * 32 + RANK, (PARTS * 32 + RANK) * h)
                             for h in range(HALVES)],
                       w_x[m][:, :, :].rearrange("p a e -> p (a e)"), 128, 0, (PARTS * 32 + RANK) * HALVES)
                yield ("w", [(w_dt_raw[m][:, h, :], 128, 128 * h) for h in range(HALVES)],
                       w_dt[m][PARTS * 32:, :], None, 0, E_IN)
                yield ("w", [(vectors_raw[m], VECTORS * HALVES, 0)], vectors[m][:, :], 128, 0, VECTORS * HALVES)
                yield ("w", [(w_out_raw[m][:, 128 * h:128 * h + 128], 128, 128 * h) for h in range(HALVES)],
                       w_out[m][:, :, :].rearrange("p a e -> p (a e)"), 128, 0, E_IN)
            for g in range(TOKENS // CHUNK):
                yield ("x", [(x_tok[:, 4 * g + a, :], 128, 128 * a) for a in range(4)],
                       x_t[:, g * CHUNK:(g + 1) * CHUNK], 128, 0, CHUNK)

        GROUPS = list(setup_groups())
        NG = len(GROUPS)

        def setup_copy(eng, copy, g, done):
            kind, parts, target, rows, lo, n = GROUPS[g]
            b = bank[SETUP_BANKS[g % 4]]
            src = b[PARTS * 32:PARTS * 32 + RANK, 0:n] if rows is None else b[:, 0:n]
            eng.wait_ge(setup_mm, g + 1)
            copy(target, src).then_inc(done, 1)

        def sign_bank(n, late):
            return bank[SETUP_BANKS[2 * n + late]][:, :].bitcast(BF16)

        @block.gpsimd
        def _(pool):
            pool.memset(ident[:, :], 0.0).then_inc(consts, 1)
            pool.memset(ident16[:, :], 0.0).then_inc(consts, 1)
            pool.memset(sel[:, :, :], 0.0).then_inc(consts, 1)
            pool.memset(ones[:, :], 1.0).then_inc(consts, 1)
            pool.wait_ge(consts, 3)
            for m in (ident, ident16):
                pool.affine_select(out=m[:, :], in_=m[:, :], compare_op=ALU.not_equal, fill=1.0, base=0,
                                   pattern=[[-1, 128]], channel_multiplier=1).then_inc(identities, 1)
            for part in range(PARTS):
                v = sel[32 * part:32 * part + 32, :, :]
                pool.wait_ge(identities, 2 + part)
                pool.affine_select(out=v, in_=v, compare_op=ALU.not_equal, fill=1.0, base=0,
                                   pattern=[[-1, BC], [0, 128]], channel_multiplier=1).then_inc(identities, 1)

            def times_b(n, i):
                if n >= LAST or n % NST not in POOL_B:
                    return
                j, m = taken(POOL_B, n), n // NST % 2
                wait(pool, u_ready, n // NST + 1, 1, i)
                wait(pool, b_copied, j + 1, len(POOL_B), i)
                wait(pool, summed, n + 1 - SLOTS, NST, i)
                pool.tensor_tensor(tile(n), u[m][:, :, :], over_halves(b_copy[:, b_slot(n), :]),
                                   ALU.mult).then_inc(input_pool, 1)

            def times_c(n, i):
                if n < 0 or n % NST not in POOL_C:
                    return
                j = taken(POOL_C, n)
                wait(pool, scanned, 2 * n + 2, 2 * NST, i)
                wait(pool, c_copied, j + 1, len(POOL_C), i)
                pool.tensor_tensor(tile(n), tile(n), over_halves(c_copy[:, c_slot(n), :]),
                                   ALU.mult).then_inc(output_pool, 1)

            def prepare(k, s, i):
                if k >= ITEMS:
                    return
                m = k % 2
                if s == AT_SPLIT + 1:
                    wait(pool, mid_ready, k + 1, 1, i)
                    pool.tensor_tensor(split[m][0:32, :], split_rest[0:32, :], split[m][0:32, :],
                                       ALU.subtract).then_inc(split_ready, 1)
                if s == AT_SUM:
                    wait(pool, lost_ready, k + 1, 1, i)
                    wait(pool, ln_ready, k + 1, 1, i)
                    pool.tensor_tensor(sp_ln[:, :, :], sp_ln[:, :, :], sp_one[:, :, :],
                                       ALU.subtract).then_inc(log1p_ready, 1)

            pool.wait_ge(identities, 2 + PARTS)
            for part in range(PARTS):
                pool.memset(pad[part][:, :, :, :], 0.0).then_inc(pads_zero, 1)
            for s in (AT_SPLIT + 1, AT_SUM):
                prepare(0, s, 0)
            times_b(0, 0)
            times_b(1, 0)

            def slot(k, s, i):
                n = NST * k + s
                times_b(n + 2, i)
                times_c(n - 1, i)
                prepare(k + 1, s, i)

            run_items(pool, slot)
            times_c(LAST - 1, 0)

        @block.scalar
        def _(act):
            def copy(o, i_):
                return act.activation(o, i_, ACT.Copy)

            act.wait_ge(load_w, W_LOADS)
            for m in range(2):
                act.activation(a_neg[m][:, :, :], a_neg[m][:, :, :], ACT.Exp).then_inc(a_exp, 1)
            for g in range(0, NG, 2):
                setup_copy(act, copy, g, setup_act)
            act.wait_ge(load_k, K_LOADS)
            for n in range(2):
                act.activation(k_sign[n][:, :], k_raw[n][:, :], ACT.Sign).then_inc(k_signed, 1)
            for n in range(2):
                act.wait_ge(setup_mm, NG + 2 * n + 1)
                copy(k_t[n][:, 0:8, :].rearrange("p a e -> p (a e)"), sign_bank(n, 0)).then_inc(setup_act, 1)

            def copy_b(n, i):
                if n >= LAST or n % NST not in POOL_B:
                    return
                wait(act, b_ready, n + 1, NST, i)
                wait(act, input_pool, earlier(POOL_B, n), len(POOL_B), i)
                copy(b_copy[:, b_slot(n), :], b_row[:, :]).then_inc(b_copied, 1)

            def copy_c(n, i):
                if n >= LAST or n % NST not in POOL_C:
                    return
                wait(act, c_ready, n + 1, NST, i)
                wait(act, output_pool, earlier(POOL_C, n), len(POOL_C), i)
                copy(c_copy[:, c_slot(n), :], c_row[:, :]).then_inc(c_copied, 1)

            def decays(n, i):
                if n >= LAST:
                    return
                m, s = n // NST % 2, n % NST
                wait(act, dt_ready, n // NST + 1, 1, i)
                for h in range(HALVES):
                    wait(act, scanned, 2 * (n - 1) + h + 1, 2 * NST, i)
                    act.activation(decay[h][:, :].rearrange("p (q l) -> p q l", l=L)[:, :, 1:],
                                   dt[m][:, h, :].rearrange("p (q l) -> p q l", l=L)[:, :, 1:],
                                   ACT.Exp, scale=a_neg[m][:, h, s:s + 1]).then_inc(decay_ready, 1)

            def prepare(k, s, i):
                if k >= ITEMS:
                    return
                m = k % 2
                mm = 7 * k
                if s == AT_PROJ:
                    for h in range(HALVES):
                        wait(act, pre_mm, mm + h + 1, 7, i)
                        wait(act, tap_done, 8 * k, 8, i)
                        act.activation(xpad[:, h, :, LPAD:], work[h][:, :].rearrange("p (q l) -> p q l", l=L),
                                       ACT.Copy).then_inc(xpad_ready, 1)
                if s == AT_SILU:
                    for h in range(HALVES):
                        wait(act, tap_done, 8 * k + 6 + h + 1, 8, i)
                        if h == 0:
                            wait(act, gated, k - 1, 1, i)
                        act.activation(xc[m][:, h, :], cv[:, h, :], ACT.Silu,
                                       bias=conv_b[m][:, h:h + 1]).then_inc(xc_ready, 1)
                    for h in range(HALVES):
                        wait(act, pre_mm, mm + 2 + h + 1, 7, i)
                        act.activation(gate[m][:, h, :], work[h][:, :], ACT.Silu).then_inc(gate_ready, 1)
                if s == AT_DBC:
                    wait(act, pre_mm, mm + 5, 7, i)
                    copy(dt_low[PARTS * 32:, :], work[0][PARTS * 32:PARTS * 32 + RANK, :]).then_inc(dt_low_ready, 1)
                    wait(act, c_ready, NST * (k - 1), NST, i)
                    copy(split[m][:, :], work[0][0:PARTS * 32, :]).then_inc(hi_ready, 1)
                if s == AT_SPLIT + 1:
                    wait(act, rest_ready, k + 1, 1, i)
                    copy(split[m][0:64, :], split_rest[:, :]).then_inc(mid_ready, 1)
                if s in (AT_DT, AT_DT + 1):
                    h = s - AT_DT
                    wait(act, pre_mm, mm + 5 + h + 1, 7, i)
                    if h == 0:
                        wait(act, dt_ready, k, 1, i)
                    src = work[1 - h]
                    act.activation(sp_e[:, h, :], src[:, :], ACT.Abs, bias=b_dt[m][:, h:h + 1]).then_inc(abs_ready, 1)
                    act.activation(sp_relu[:, h, :], src[:, :], ACT.Relu,
                                   bias=b_dt[m][:, h:h + 1]).then_inc(relu_ready, 1)
                if s == AT_EXP:
                    wait(act, abs_ready, 2 * k + 2, 2, i)
                    act.activation(sp_e[:, :, :], sp_e[:, :, :], ACT.Exp, scale=-1.0).then_inc(exp_ready, 1)
                if s == AT_LN:
                    wait(act, exp_ready, k + 1, 1, i)
                    act.activation(sp_one[:, :, :], sp_e[:, :, :], ACT.Identity, bias=1.0).then_inc(one_ready, 1)
                    act.activation(sp_ln[:, :, :], sp_e[:, :, :], ACT.Ln, bias=1.0).then_inc(ln_ready, 1)

            for s in range(NST):
                prepare(0, s, 0)
            copy_b(0, 0)
            copy_b(1, 0)
            act.wait_ge(a_ready, 2)
            act.wait_ge(zeros, 6)
            decays(0, 0)

            def slot(k, s, i):
                n = NST * k + s
                copy_b(n + 2, i)
                copy_c(n, i)
                decays(n + 1, i)
                prepare(k + 1, s, i)

            run_items(act, slot)

            for layer in range(2):
                act.wait_ge(bn_mv, layer + 1)
                if layer == 0:
                    act.activation(bn_tmp[:, 0:1], mv[:, 1:2], ACT.Sqrt, bias=eps[:, 0:1]).then_inc(bn_std, 1)
                else:
                    act.activation(bn_tmp[:, 0:1], mv[:, 1:2], ACT.Sqrt, bias=eps[:, 0:1],
                                   scale=k_mean_sq[:, 0:1]).then_inc(bn_std, 1)
                act.wait_ge(bn_ready, layer + 1)
                for n in range(TILES):
                    b, half = n // 2, n % 2
                    src = (res[:, b, half * CHUNK:(half + 1) * CHUNK] if layer == 0 else bank[n][:, :])
                    src3 = src.rearrange("p (r w) -> p r w", w=W)
                    if layer == 0 and n == 0:
                        act.wait_ge(pads_zero, PARTS)
                    act.activation(inner(0, n), src3, ACT.Relu, bias=bn_b[layer][:, 0:1],
                                   scale=bn_a[layer][:, 0:1]).then_inc(act_hi, 1)
                    g = TILES * layer + n
                    if g >= 2:
                        act.wait_ge(act_rest, g - 1)
                    act.activation(act_f[:, n % 2, :], src, ACT.Relu, bias=bn_b[layer][:, 0:1],
                                   scale=bn_a[layer][:, 0:1]).then_inc(act_full, 1)

        @block.vector
        def _(dve):
            for m in range(2):
                dve.memset(w_dt_raw[m][:, :, 0:PARTS * 32], 0.0).then_inc(zeros, 1)
            dve.memset(xpad[:, :, :, 0:LPAD], 0.0).then_inc(zeros, 1)
            for h in range(HALVES):
                dve.memset(decay[h][:, :].rearrange("p (q l) -> p q l", l=L)[:, :, 0:1], 0.0).then_inc(zeros, 1)
            dve.memset(eps[:, :], EPS).then_inc(zeros, 1)
            for m in range(2):
                dve.wait_ge(a_exp, m + 1)
                dve.tensor_scalar(a_neg[m][:, :, :], a_neg[m][:, :, :], -1.0, None, ALU.mult).then_inc(a_ready, 1)
            for g in range(1, NG, 2):
                setup_copy(dve, dve.tensor_copy, g, setup_dve)
            dve.wait_ge(load_k, K_LOADS)
            for n in range(2):
                dve.tensor_reduce(k_abs[:, n:n + 1], k_raw[n][:, :], AX.X, ALU.add,
                                  apply_absolute_value=True).then_inc(k_summed, 1)
            for n in range(2):
                dve.wait_ge(setup_mm, NG + 2 * n + 2)
                dve.tensor_copy(k_t[n][:, 8, :], sign_bank(n, 1)[:, 0:128]).then_inc(setup_dve, 1)
            dve.wait_ge(k_mean_mm, 1)
            dve.tensor_scalar(k_mean[:, :], b_row[:, 0:2], 1.0 / WCOUNT, None, ALU.mult).then_inc(k_mean_ready, 1)
            dve.wait_ge(k_mean_ready, 1)
            dve.tensor_tensor(k_mean_sq[:, :], k_mean[:, :], k_mean[:, :], ALU.mult).then_inc(k_mean_ready, 1)

            def times_b(n, i):
                if n >= LAST or n % NST in POOL_B:
                    return
                wait(dve, u_ready, n // NST + 1, 1, i)
                wait(dve, b_ready, n + 1, NST, i)
                wait(dve, summed, n + 1 - SLOTS, NST, i)
                dve.tensor_tensor(tile(n), u[n // NST % 2][:, :, :], over_halves(b_row[:, :]),
                                  ALU.mult).then_inc(input_dve, 1)

            def scan(n, i):
                wait_input(dve, n, i)
                for h in range(HALVES):
                    wait(dve, decay_ready, 2 * n + h + 1, 2 * NST, i)
                    dve.tensor_tensor_scan(tile(n)[:, h, :], decay[h][:, :], tile(n)[:, h, :], 0.0,
                                           ALU.mult, ALU.add).then_inc(scanned, 1)

            def times_c(n, i):
                if n < 0 or n % NST in POOL_C:
                    return
                wait(dve, scanned, 2 * n + 2, 2 * NST, i)
                wait(dve, c_ready, n + 1, NST, i)
                dve.tensor_tensor(tile(n), tile(n), over_halves(c_row[:, :]), ALU.mult).then_inc(output_dve, 1)

            def prepare(k, s, i):
                if k >= ITEMS:
                    return
                m = k % 2
                if AT_CONV <= s < AT_CONV + KCONV:
                    tap = s - AT_CONV
                    for h in range(HALVES):
                        src = xpad[:, h, :, tap:tap + L]
                        acc = cv[:, h, :].rearrange("p (q l) -> p q l", l=L)
                        w = conv_w[m][:, h, tap:tap + 1]
                        if tap == 0:
                            wait(dve, xpad_ready, 2 * k + h + 1, 2, i)
                            wait(dve, xc_ready, 2 * k, 2, i)
                            dve.tensor_scalar(acc, src, w, None, ALU.mult).then_inc(tap_done, 1)
                        else:
                            wait(dve, tap_done, 8 * k + 2 * (tap - 1) + h + 1, 8, i)
                            dve.scalar_tensor_tensor(acc, src, w, acc, ALU.mult, ALU.add).then_inc(tap_done, 1)
                if s == AT_SPLIT:
                    wait(dve, hi_ready, k + 1, 1, i)
                    wait(dve, split_ready, k, 1, i)
                    dve.tensor_tensor(split_rest[:, :], work[0][0:64, :], split[m][0:64, :],
                                      ALU.subtract).then_inc(rest_ready, 1)
                if s == AT_RES:
                    wait(dve, one_ready, k + 1, 1, i)
                    dve.scalar_tensor_tensor(sp_one[:, :, :], sp_one[:, :, :], 1.0, sp_e[:, :, :],
                                             ALU.subtract, ALU.subtract).then_inc(lost_ready, 1)
                if s == AT_SUM:
                    wait(dve, log1p_ready, k + 1, 1, i)
                    wait(dve, relu_ready, 2 * k + 2, 2, i)
                    wait(dve, decay_ready, 2 * NST * (k - 1), 2 * NST, i)
                    dve.tensor_tensor(dt[m][:, :, :], sp_ln[:, :, :], sp_relu[:, :, :], ALU.add).then_inc(dt_ready, 1)
                    wait(dve, dt_ready, k + 1, 1, i)
                    wait(dve, xc_ready, 2 * k + 2, 2, i)
                    wait(dve, scanned, 2 * NST * (k - 1), 2 * NST, i)
                    dve.tensor_tensor(u[m][:, :, :], dt[m][:, :, :], xc[m][:, :, :], ALU.mult).then_inc(u_ready, 1)

            def post(k, i):
                m, j = k % 2, k // 2 % 2
                wait(dve, summed, NST * (k + 1), NST, i)
                for h in range(HALVES):
                    dve.scalar_tensor_tensor(xc[m][:, h, :], xc[m][:, h, :], d_skip[m][:, h:h + 1],
                                             y_sum[h][:, :], ALU.mult, ALU.add).then_inc(y_read, 1)
                wait(dve, y_read, 2 * k + 2, 2, i)
                wait(dve, gate_ready, 2 * k + 2, 2, i)
                dve.tensor_tensor(y_gated[:, 2 * m:2 * m + 2, j * CHUNK:(j + 1) * CHUNK], xc[m][:, :, :],
                                  gate[m][:, :, :], ALU.mult).then_inc(gated, 1)

            def add_output(k, part, i):
                b = k // ITEMS_PER_IMAGE - 1 + i
                wait_image(dve, out_mm, 2 * (k // ITEMS_PER_IMAGE - 1) + part + 1, i)
                dst = res[:, bass.ds(b, 1), part * CHUNK:(part + 1) * CHUNK].rearrange("p b n -> p (b n)")
                dve.tensor_tensor(dst, dst, work[1 - part][:, :], ALU.add).then_inc(res_added, 1)

            for s in range(NST):
                prepare(0, s, 0)
            dve.wait_ge(load_res, 16 * NB)
            times_b(0, 0)

            def slot(k, s, i):
                n = NST * k + s
                times_b(n + 1, i)
                scan(n, i)
                times_c(n - 1, i)
                if s == AT_POST and k > 0:
                    post(k - 1, i)
                if k % ITEMS_PER_IMAGE == 0 and k > 0 and s == AT_OUT + 4:
                    add_output(k, 0, i)
                prepare(k + 1, s, i)
                if k % ITEMS_PER_IMAGE == 0 and k > 0 and s == NST - 1:
                    add_output(k, 1, i)

            run_items(dve, slot)
            times_c(LAST - 1, 0)
            post(ITEMS - 1, 0)
            for part in range(2):
                add_output(ITEMS, part, 0)

            for layer in range(2):
                for n in range(TILES):
                    b, half = n // 2, n % 2
                    if layer == 0:
                        if n == 0:
                            dve.wait_ge(res_added, 2 * NB)
                        src = res[:, b, half * CHUNK:(half + 1) * CHUNK]
                    else:
                        dve.wait_ge(conv_mm, n + 1)
                        src = bank[n][:, :]
                    dve.bn_stats(stats[:, n, :], src).then_inc(stat_done, 1)
                dve.wait_ge(stat_done, TILES * (layer + 1))
                dve.bn_aggr(mv[:, :], stats[:, :, :].rearrange("p a b -> p (a b)")).then_inc(bn_mv, 1)
                dve.wait_ge(bn_std, layer + 1)
                q = 3 * layer
                dve.reciprocal(bn_tmp[:, 1:2], bn_tmp[:, 0:1]).then_inc(bn_step, 1)
                dve.wait_ge(bn_step, q + 1)
                if layer == 0:
                    dve.tensor_tensor(bn_a[0][:, :], bn_tmp[:, 1:2], gamma[0][:, :], ALU.mult).then_inc(bn_step, 1)
                else:
                    dve.scalar_tensor_tensor(bn_a[1][:, :], bn_tmp[:, 1:2], k_mean[:, 0:1], gamma[1][:, :],
                                             ALU.mult, ALU.mult).then_inc(bn_step, 1)
                dve.wait_ge(bn_step, q + 2)
                dve.wait_ge(bn_mv, layer + 1)
                dve.tensor_tensor(bn_tmp[:, 2:3], mv[:, 0:1], bn_a[layer][:, :], ALU.mult).then_inc(bn_step, 1)
                dve.wait_ge(bn_step, q + 3)
                dve.tensor_tensor(bn_b[layer][:, :], beta[layer][:, :], bn_tmp[:, 2:3],
                                  ALU.subtract).then_inc(bn_ready, 1)
                for n in range(TILES):
                    g = TILES * layer + n
                    rest = act_r[:, n % 2, :].rearrange("p (r w) -> p r w", w=W)
                    full = act_f[:, n % 2, :].rearrange("p (r w) -> p r w", w=W)
                    dve.wait_ge(act_full, g + 1)
                    dve.wait_ge(act_hi, g + 1)
                    if g >= 2:
                        dve.wait_ge(act_lo, g - 1)
                    dve.tensor_tensor(rest, full, inner(0, n), ALU.subtract).then_inc(act_rest, 1)
                    dve.wait_ge(act_rest, g + 1)
                    dve.tensor_copy(inner(1, n), rest).then_inc(act_mid, 1)
                    dve.wait_ge(act_mid, g + 1)
                    dve.tensor_tensor(inner(2, n), rest, inner(1, n), ALU.subtract).then_inc(act_lo, 1)
            for n in range(TILES):
                b, half = n // 2, n % 2
                dst = res[:, b, half * CHUNK:(half + 1) * CHUNK]
                dve.wait_ge(conv_mm, TILES + n + 1)
                dve.scalar_tensor_tensor(dst, bank[n][:, :], k_mean[:, 1:2], dst,
                                         ALU.mult, ALU.add).then_inc(y_ready, 1)

        @block.tensor
        def _(pe):
            pe.wait_ge(identities, 2 + PARTS)
            pe.wait_ge(consts, 4)
            pe.wait_ge(zeros, 2)
            pe.wait_ge(load_w, W_LOADS)
            groups_x = 0
            for g, (kind, parts, _, _, _, _) in enumerate(GROUPS):
                if g >= 4:
                    if g % 2 == 0:
                        pe.wait_ge(setup_act, (g - 4) // 2 + 1)
                    else:
                        pe.wait_ge(setup_dve, (g - 4) // 2 + 1)
                if kind == "x":
                    pe.wait_ge(load_x, 16 * (groups_x // 2 + 1))
                    groups_x += 1
                for src, cols, at in parts:
                    rows = src.shape[0]
                    b = bank[SETUP_BANKS[g % 4]]
                    mm = pe.transpose(b[0:src.shape[1], at:at + rows], src, ident[0:rows, 0:rows])
                mm.then_inc(setup_mm, 1)
            pe.wait_ge(k_signed, 2)
            pe.wait_ge(setup_act, NG // 2)
            pe.wait_ge(setup_dve, NG // 2)
            for n in range(2):
                taps = k_sign[n][:, :].rearrange("p (i q) -> p q i", q=TAPS)
                for q in range(8):
                    mm = pe.transpose(sign_bank(n, 0)[:, 128 * q:128 * q + 128], taps[:, q, :], ident16[:, :])
                mm.then_inc(setup_mm, 1)
                pe.transpose(sign_bank(n, 1)[:, 0:128], taps[:, 8, :], ident16[:, :]).then_inc(setup_mm, 1)
            pe.wait_ge(k_summed, 2)
            pe.matmul(b_row[:, 0:2], ones[:, :], k_abs[:, :]).then_inc(k_mean_mm, 1)

            def spread(row, n, ready, i):
                wait(pe, split_ready, n // NST + 1, 1, i)
                target = b_row if row < NST else c_row
                pe.matmul(target[:, :], sel[:, row, :], split[n // NST % 2][:, :]).then_inc(ready, 1)

            def spread_b(n, i):
                if n >= LAST:
                    return
                if (n - 1) % NST in POOL_B:
                    wait(pe, b_copied, taken(POOL_B, n), len(POOL_B), i)
                elif n > 0:
                    wait(pe, input_dve, n - taken(POOL_B, n), NST - len(POOL_B), i)
                spread(n % NST, n, b_ready, i)

            def spread_c(n, i):
                if (n - 1) % NST in POOL_C:
                    wait(pe, c_copied, taken(POOL_C, n), len(POOL_C), i)
                elif n > 0:
                    wait(pe, output_dve, n - taken(POOL_C, n), NST - len(POOL_C), i)
                spread(NST + n % NST, n, c_ready, i)

            def sum_states(n, i):
                if n < 0:
                    return
                wait_output(pe, n, i)
                if n % NST == 0:
                    wait(pe, y_read, 2 * (n // NST), 2, i)
                for h in range(HALVES):
                    mm = pe.matmul(y_sum[h][:, :], ident[:, :], tile(n)[:, h, :],
                                   start=(n % NST == 0), stop=(n % NST == NST - 1))
                mm.then_inc(summed, 1)

            def prepare(k, s, i):
                if k >= ITEMS:
                    return
                m = k % 2
                moving = x_t[:, bass.ds(k // 2 * CHUNK + i * (2 * CHUNK), CHUNK)]
                if s == AT_PROJ:
                    for h in range(HALVES):
                        wait(pe, relu_ready, 2 * k if h == 0 else 2 * k - 1, 2, i)
                        pe.matmul(work[h][:, :], w_in[m][:, h, :], moving).then_inc(pre_mm, 1)
                if s == AT_SILU:
                    for h in range(HALVES):
                        wait(pe, xpad_ready, 2 * k + h + 1, 2, i)
                        pe.matmul(work[h][:, :], w_in[m][:, HALVES + h, :], moving).then_inc(pre_mm, 1)
                if s == AT_DBC:
                    wait(pe, gate_ready, 2 * k + 1, 2, i)
                    wait(pe, xc_ready, 2 * k + 2, 2, i)
                    for h in range(HALVES):
                        mm = pe.matmul(work[0][0:PARTS * 32 + RANK, :], w_x[m][:, h, :], xc[m][:, h, :],
                                       start=(h == 0), stop=(h == HALVES - 1))
                    mm.then_inc(pre_mm, 1)
                if s == AT_DT:
                    wait(pe, dt_low_ready, k + 1, 1, i)
                    for h in range(HALVES):
                        if h == 0:
                            wait(pe, gate_ready, 2 * k + 2, 2, i)
                        else:
                            wait(pe, rest_ready, k + 1, 1, i)
                        pe.matmul(work[1 - h][:, :], w_dt[m][PARTS * 32:, 128 * h:128 * h + 128],
                                  dt_low[PARTS * 32:, :]).then_inc(pre_mm, 1)

            def project_out(k, r, i):
                part, q = r // 4, r % 4
                if r == 0:
                    wait(pe, gated, k, 1, i)
                    if k < ITEMS:
                        wait(pe, relu_ready, 2 * (k + 1) + 2, 2, i)
                for g in range(4):
                    mm = pe.matmul(work[1 - part][:, 128 * q:128 * q + 128],
                                   y_gated[:, g, r:HW:8], w_out[g // 2][:, g % 2, :],
                                   start=(g == 0), stop=(g == 3), skip_group_check=True)
                if q == 3:
                    mm.then_inc(out_mm, 1)

            pe.wait_ge(k_mean_ready, 1)
            pe.wait_ge(setup_act, NG // 2 + 2)
            pe.wait_ge(setup_dve, NG // 2 + 2)
            for s in range(NST):
                prepare(0, s, 0)
            spread_b(0, 0)
            spread_b(1, 0)

            def slot(k, s, i):
                n = NST * k + s
                spread_b(n + 2, i)
                spread_c(n, i)
                sum_states(n - LAG, i)
                if k % ITEMS_PER_IMAGE == 0 and k > 0 and s >= AT_OUT:
                    project_out(k, s - AT_OUT, i)
                prepare(k + 1, s, i)
                if k % ITEMS_PER_IMAGE == 0 and k > 0 and s == NST - 1:
                    wait_image(pe, res_added, 2 * (k // ITEMS_PER_IMAGE), i)

            run_items(pe, slot)
            for n in range(LAST - LAG, LAST):
                sum_states(n, 0)
            for r in range(8):
                project_out(ITEMS, r, 0)

            for layer in range(2):
                for n in range(TILES):
                    b, r = n // 2, ROWS * (n % 2)
                    if n % 2 == 0:
                        pe.wait_ge(act_lo, TILES * layer + n + 2)
                    for q in range(TAPS):
                        for part in range(PARTS):
                            src = pad[part][:, b, r + q // 3:r + q // 3 + ROWS, q % 3:q % 3 + W]
                            mm = pe.matmul(bank[n][:, :].rearrange("p (r w) -> p r w", w=W), k_t[layer][:, q, :], src,
                                           start=(q == 0 and part == 0), stop=(q == TAPS - 1 and part == PARTS - 1))
                    mm.then_inc(conv_mm, 1)


_INS = ['x'] + [f'L0_conv_{n}{m}' for m in (1, 2) for n in
                ('W_in', 'conv_w', 'conv_b', 'W_x', 'W_dt', 'b_dt', 'A_log', 'D_skip', 'W_out')] + \
       [f'L1_conv_{n}' for n in ('gamma0', 'beta0', 'w0', 'gamma1', 'beta1', 'w1')]


def kernel(**inputs):
    import numpy as _np
    import concourse.bacc as _bacc
    from concourse import mybir as _mybir
    from concourse.bass_utils import run_bass_kernel_spmd as _run

    nc = _bacc.Bacc("TRN2", target_bir_lowering=False, num_devices=1)
    arrays, tensors = {}, {}
    for name in _INS:
        a = _np.ascontiguousarray(inputs[name])
        arrays[f"in_{name}_dram"] = a
        tensors[name] = nc.dram_tensor(f"in_{name}_dram", a.shape, _mybir.dt.from_np(a.dtype),
                                       kind="ExternalInput").ap()
    out = nc.dram_tensor("out_0_dram", (NB, C, H, W), F32, kind="ExternalOutput").ap()
    mamba_conv_kernel(nc, tensors, out)
    r = _run(nc, [arrays], core_ids=[0])
    return r.results[0]["out_0_dram"]
```

```python
from contextlib import ExitStack

import concourse.bass as bass
from concourse import mybir

ALU = mybir.AluOpType
ACT = mybir.ActivationFunctionType
AX = mybir.AxisListType
F32 = mybir.dt.float32
BF16 = mybir.dt.bfloat16

NB, C, H, W = 4, 128, 32, 32
HW = H * W
D = C
L = W
E_IN = 2 * D
HALVES = E_IN // 128
NST = 16
RANK = D // 16
VECTORS = 3
KCONV = 4
TOKENS = NB * HW
CHUNK = 512
CSEQ = CHUNK // L
MAMBAS = 2
CHUNKS_PER_IMAGE = HW // CHUNK
ITEMS_PER_IMAGE = CHUNKS_PER_IMAGE * MAMBAS
ITEMS = NB * ITEMS_PER_IMAGE
BC = 2 * NST
PARTS = 3
LPAD = KCONV - 1
TAPS = 9
EPS = 1e-5
HP, WP = H + 2, W + 2
TILES = NB * 2
ROWS = H // 2
WCOUNT = C * C * TAPS

SLOTS = 8
LAG = 3
LEAD = 4
B_COPIES, C_COPIES = 4, 2
DECAYS = 3

POOL_C = (0, 2, 9, 11)

AT_PROJ = NST - HALVES
AT_TAPS = (0, 1, 2, 4)
AT_POST = LAG
AT_GATE = 4
AT_SILU = 5
AT_DBC = 6
AT_REST, AT_MID, AT_LOW = 7, 7, 8
AT_DT = 7
AT_EXP, AT_LN, AT_LOST, AT_LOG1P, AT_U = 9, 10, 11, 11, 12
AT_OUT = 9


def mamba_conv_kernel(nc, t, out):
    x = t["x"]
    ctx = ExitStack()
    with ctx:
        def sb(name, shape, dt=F32):
            return ctx.enter_context(nc.sbuf_tensor(name, shape, dt))

        def sem(name):
            return ctx.enter_context(nc.semaphore(name))

        ident = sb("ident", [128, 128])
        ident16 = sb("ident16", [128, 128], BF16)
        ones = sb("ones", [128, 128])
        sel = sb("sel", [PARTS * 32, BC, 128], BF16)
        eps = sb("eps", [128, 1])
        state = sb("state", [128, SLOTS, HALVES, CHUNK])
        raw = state[:, :, :, :].rearrange("p a h n -> p (a h n)")
        raw_used = [0]

        def staged(columns):
            raw_used[0] += columns
            assert raw_used[0] <= SLOTS * HALVES * CHUNK
            return raw[:, raw_used[0] - columns:raw_used[0]]

        XROWS = PARTS * 32 + RANK
        w_in_raw = [staged(4 * 128).rearrange("p (a d) -> p a d", a=4) for m in range(2)]
        w_x_raw = [staged(E_IN)[0:XROWS, :] for m in range(2)]
        w_dt_raw = [staged(HALVES * XROWS).rearrange("p (a r) -> p a r", a=HALVES) for m in range(2)]
        w_out_raw = [staged(E_IN) for m in range(2)]
        vectors_raw = [staged(128)[0:VECTORS * HALVES, :] for m in range(2)]
        k_raw = [staged(C * TAPS) for n in range(2)]
        k_sign = [staged(C * TAPS // 2).bitcast(BF16) for n in range(2)]
        w_in = [sb(f"w_in{m}", [128, 4, 128]) for m in range(2)]
        w_x = [sb(f"w_x{m}", [128, HALVES, PARTS * 32 + RANK]) for m in range(2)]
        w_dt = [sb(f"w_dt{m}", [PARTS * 32 + RANK, E_IN]) for m in range(2)]
        w_out = [sb(f"w_out{m}", [128, HALVES, 128]) for m in range(2)]
        conv_w = [sb(f"conv_w{m}", [128, HALVES, KCONV]) for m in range(2)]
        vectors = [sb(f"vectors{m}", [128, VECTORS * HALVES]) for m in range(2)]
        conv_b, b_dt, d_skip = ([vectors[m][:, HALVES * v:HALVES * v + HALVES] for m in range(2)]
                                for v in range(VECTORS))
        a_neg = [sb(f"a_neg{m}", [128, HALVES, NST]) for m in range(2)]
        k_t = [sb(f"k_t{n}", [128, TAPS, 128], BF16) for n in range(2)]
        k_abs = sb("k_abs", [128, 2])
        k_mean = sb("k_mean", [128, 2])
        k_mean_sq = sb("k_mean_sq", [128, 2])
        gamma = [sb(f"gamma{n}", [128, 1]) for n in range(2)]
        beta = [sb(f"beta{n}", [128, 1]) for n in range(2)]

        x_tok = sb("x_tok", [128, TOKENS // 128, 128])
        y_gated = x_tok[:, :, :].rearrange("p a d -> p (a d)").rearrange("p (g n) -> p g n", g=4)
        x_t = sb("x_t", [128, TOKENS])
        res = sb("res", [128, NB, HW])
        xpad = sb("xpad", [128, HALVES, CSEQ, LPAD + L])
        cv = sb("cv", [128, HALVES, CHUNK])
        xc = [sb(f"xc{m}", [128, HALVES, CHUNK]) for m in range(2)]
        gate = [sb(f"gate{m}", [128, HALVES, CHUNK]) for m in range(2)]
        dt = [sb(f"dt{m}", [128, HALVES, CHUNK]) for m in range(2)]
        u = [sb(f"u{m}", [128, HALVES, CHUNK]) for m in range(2)]
        split = [sb(f"split{m}", [PARTS * 32, CHUNK], BF16) for m in range(2)]
        split_rest = sb("split_rest", [64, CHUNK])
        dt_low = sb("dt_low", [PARTS * 32 + RANK, CHUNK])
        sp_e = sb("sp_e", [128, HALVES, CHUNK])
        sp_relu = sb("sp_relu", [128, HALVES, CHUNK])
        sp_ln = sb("sp_ln", [128, HALVES, CHUNK])
        sp_one = sb("sp_one", [128, HALVES, CHUNK])
        b_copy = sb("b_copy", [128, B_COPIES, CHUNK])
        c_copy = sb("c_copy", [128, C_COPIES, CHUNK])
        pad = [sb(f"pad{p}", [128, NB, HP, WP], BF16) for p in range(PARTS)]
        act_f, act_r = b_copy[:, 0:2, :], b_copy[:, 2:4, :]
        stats = sb("stats", [128, TILES, 6])
        mv = sb("mv", [128, 2])
        bn_tmp = sb("bn_tmp", [128, 4])
        bn_a = [sb(f"bn_a{n}", [128, 1]) for n in range(2)]
        bn_b = [sb(f"bn_b{n}", [128, 1]) for n in range(2)]

        bank = [ctx.enter_context(nc.psum_tensor(f"bank{i}", [128, CHUNK], F32)) for i in range(8)]
        decay = bank[0:DECAYS]
        b_row, c_row = bank[3], bank[4]
        y_sum = bank[5:7]
        work = bank[7]

        load_w = sem("load_w")
        load_x = sem("load_x")
        load_res = sem("load_res")
        load_k = sem("load_k")
        consts = sem("consts")
        zeros = sem("zeros")
        pads_zero = sem("pads_zero")
        identities = sem("identities")
        a_exp = sem("a_exp")
        a_ready = sem("a_ready")
        k_signed = sem("k_signed")
        k_summed = sem("k_summed")
        k_mean_mm = sem("k_mean_mm")
        k_mean_ready = sem("k_mean_ready")
        setup_mm = sem("setup_mm")
        setup_act = sem("setup_act")
        setup_dve = sem("setup_dve")
        pre_mm = sem("pre_mm")
        xpad_ready = sem("xpad_ready")
        tap_done = sem("tap_done")
        xc_ready = sem("xc_ready")
        gate_ready = sem("gate_ready")
        dt_low_ready = sem("dt_low_ready")
        hi_ready = sem("hi_ready")
        rest_ready = sem("rest_ready")
        mid_ready = sem("mid_ready")
        split_ready = sem("split_ready")
        abs_ready = sem("abs_ready")
        relu_ready = sem("relu_ready")
        exp_ready = sem("exp_ready")
        ln_ready = sem("ln_ready")
        one_ready = sem("one_ready")
        lost_ready = sem("lost_ready")
        log1p_ready = sem("log1p_ready")
        dt_ready = sem("dt_ready")
        u_ready = sem("u_ready")
        b_ready = sem("b_ready")
        c_ready = sem("c_ready")
        b_copied = sem("b_copied")
        c_copied = sem("c_copied")
        decay_ready = sem("decay_ready")
        input_ready = sem("input_ready")
        scanned = sem("scanned")
        output_dve = sem("output_dve")
        output_pool = sem("output_pool")
        summed = sem("summed")
        y_read = sem("y_read")
        gated = sem("gated")
        out_mm = sem("out_mm")
        res_added = sem("res_added")
        stat_done = sem("stat_done")
        bn_mv = sem("bn_mv")
        bn_std = sem("bn_std")
        bn_step = sem("bn_step")
        bn_ready = sem("bn_ready")
        act_hi = sem("act_hi")
        act_full = sem("act_full")
        act_rest = sem("act_rest")
        act_mid = sem("act_mid")
        act_lo = sem("act_lo")
        conv_mm = sem("conv_mm")
        y_ready = sem("y_ready")
        y_stored = sem("y_stored")

        block = ctx.enter_context(nc.Block())

        def wait(eng, semaphore, count, per_item, i):
            if count > 0:
                eng.wait_ge(semaphore, count + i * (per_item * ITEMS_PER_IMAGE))

        def wait_image(eng, semaphore, count, i):
            if count > 0:
                eng.wait_ge(semaphore, count + i * 2)

        def taken(states, n):
            return n // NST * len(states) + sum(s < n % NST for s in states)

        def run_items(eng, slot):
            for s in range(NST):
                slot(0, s, 0)
            with eng.Fori(0, NB - 1) as i:
                for k in range(1, ITEMS_PER_IMAGE + 1):
                    for s in range(NST):
                        slot(k, s, i)
            for k in range(ITEMS - ITEMS_PER_IMAGE + 1, ITEMS):
                for s in range(NST):
                    slot(k, s, 0)

        LAST = ITEMS * NST

        def wait_output(eng, n, i):
            if n % NST in POOL_C:
                wait(eng, output_pool, taken(POOL_C, n) + 1, len(POOL_C), i)
            else:
                wait(eng, output_dve, n - taken(POOL_C, n) + 1, NST - len(POOL_C), i)

        def c_slot(n):
            return taken(POOL_C, n) % C_COPIES

        def decay_bank(n, h):
            return decay[(HALVES * (n % NST) + h) % DECAYS]

        def decay_free(n, h):
            j, before = HALVES * (n % NST) + h, HALVES * NST * (n // NST)
            if j >= DECAYS:
                return before + j - DECAYS + 1
            return before - HALVES * NST + max(q for q in range(HALVES * NST) if q % DECAYS == j) + 1

        def inner(part, n):
            b, r = n // 2, ROWS * (n % 2)
            return pad[part][:, b, 1 + r:1 + r + ROWS, 1:1 + W]

        def tile(n):
            return state[:, n % SLOTS, :, :]

        def over_halves(row):
            return row.unsqueeze(1).to_broadcast([128, HALVES, CHUNK])

        SETUP_BANKS = (4, 5, 6, 7)

        @block.sync
        def _(sp):
            for m in range(2):
                s = str(m + 1)
                sp.dma_start(w_in_raw[m][:, :, :],
                             t[f"L0_conv_W_in{s}"].rearrange("(a p) d -> p a d", p=128)).then_inc(load_w, 16)
                if m == 0:
                    rows = x.rearrange("b c h w -> (b c h w)").rearrange("(a p d) -> p a d", p=128, d=D)
                    for q in range(4):
                        n = TOKENS // 128 // 4
                        sp.dma_start(x_tok[:, q * n:(q + 1) * n, :],
                                     rows[:, q * n:(q + 1) * n, :]).then_inc(load_x, 16)
                w = t[f"L0_conv_W_x{s}"]
                for part in range(PARTS):
                    sp.dma_start(w_x_raw[m][32 * part:32 * part + 32, :], w[RANK:RANK + BC, :]).then_inc(load_w, 16)
                sp.dma_start(w_x_raw[m][PARTS * 32:PARTS * 32 + RANK, :], w[0:RANK, :]).then_inc(load_w, 16)
                sp.dma_start(w_out_raw[m][:, :], t[f"L0_conv_W_out{s}"]).then_inc(load_w, 16)
                sp.wait_ge(zeros, 2)
                sp.dma_start(w_dt_raw[m][:, :, PARTS * 32:],
                             t[f"L0_conv_W_dt{s}"].rearrange("(a p) r -> p a r", p=128)).then_inc(load_w, 16)
                sp.dma_start(conv_w[m][:, :, :],
                             t[f"L0_conv_conv_w{s}"].rearrange("(a p) k -> p a k", p=128)).then_inc(load_w, 16)
                sp.dma_start(a_neg[m][:, :, :],
                             t[f"L0_conv_A_log{s}"].rearrange("(a p) n -> p a n", p=128)).then_inc(load_w, 16)
                for v, name in enumerate(("conv_b", "b_dt", "D_skip")):
                    sp.dma_start(vectors_raw[m][HALVES * v:HALVES * v + HALVES, :],
                                 t[f"L0_conv_{name}{s}"].rearrange("(a p) -> a p", p=128)).then_inc(load_w, 16)
            for n in range(2):
                sp.dma_start(k_raw[n][:, :], t[f"L1_conv_w{n}"].rearrange("o i a b -> o (i a b)")).then_inc(load_k, 16)
                sp.dma_start(gamma[n][:, :], t[f"L1_conv_gamma{n}"].rearrange("(p a) -> p a", a=1)).then_inc(load_k, 16)
                sp.dma_start(beta[n][:, :], t[f"L1_conv_beta{n}"].rearrange("(p a) -> p a", a=1)).then_inc(load_k, 16)
            for b in range(NB):
                sp.dma_start(res[:, b, :], x[b].rearrange("c h w -> c (h w)")).then_inc(load_res, 16)
            for n in range(TILES):
                sp.wait_ge(y_ready, n + 1)
                b, half = n // 2, n % 2
                sp.dma_start(out[b].rearrange("c h w -> c (h w)")[:, half * CHUNK:(half + 1) * CHUNK],
                             res[:, b, half * CHUNK:(half + 1) * CHUNK]).then_inc(y_stored, 16)
            sp.wait_ge(y_stored, 16 * TILES)

        W_LOADS = 16 * MAMBAS * (1 + PARTS + 1 + 1 + 1 + 1 + 1 + 3)
        K_LOADS = 16 * 2 * 3

        def setup_groups():
            for m in range(2):
                yield ("w", [(w_in_raw[m][:, a, :], 128, 128 * a) for a in range(4)],
                       w_in[m][:, :, :].rearrange("p a e -> p (a e)"), 128, 0, 512)
                yield ("w", [(w_x_raw[m][:, 128 * h:128 * h + 128], PARTS * 32 + RANK, (PARTS * 32 + RANK) * h)
                             for h in range(HALVES)],
                       w_x[m][:, :, :].rearrange("p a e -> p (a e)"), 128, 0, (PARTS * 32 + RANK) * HALVES)
                yield ("w", [(w_dt_raw[m][:, h, :], 128, 128 * h) for h in range(HALVES)],
                       w_dt[m][PARTS * 32:, :], None, 0, E_IN)
                yield ("w", [(vectors_raw[m], VECTORS * HALVES, 0)], vectors[m][:, :], 128, 0, VECTORS * HALVES)
                yield ("w", [(w_out_raw[m][:, 128 * h:128 * h + 128], 128, 128 * h) for h in range(HALVES)],
                       w_out[m][:, :, :].rearrange("p a e -> p (a e)"), 128, 0, E_IN)
            for g in range(TOKENS // CHUNK):
                yield ("x", [(x_tok[:, 4 * g + a, :], 128, 128 * a) for a in range(4)],
                       x_t[:, g * CHUNK:(g + 1) * CHUNK], 128, 0, CHUNK)

        GROUPS = list(setup_groups())
        NG = len(GROUPS)

        def setup_copy(eng, copy, g, done):
            kind, parts, target, rows, lo, n = GROUPS[g]
            b = bank[SETUP_BANKS[g % 4]]
            src = b[PARTS * 32:PARTS * 32 + RANK, 0:n] if rows is None else b[:, 0:n]
            eng.wait_ge(setup_mm, g + 1)
            copy(target, src).then_inc(done, 1)

        def sign_bank(n, late):
            return bank[SETUP_BANKS[2 * n + late]][:, :].bitcast(BF16)

        @block.gpsimd
        def _(pool):
            pool.memset(ident[:, :], 0.0).then_inc(consts, 1)
            pool.memset(ident16[:, :], 0.0).then_inc(consts, 1)
            pool.memset(sel[:, :, :], 0.0).then_inc(consts, 1)
            pool.memset(ones[:, :], 1.0).then_inc(consts, 1)
            pool.wait_ge(consts, 3)
            for m in (ident, ident16):
                pool.affine_select(out=m[:, :], in_=m[:, :], compare_op=ALU.not_equal, fill=1.0, base=0,
                                   pattern=[[-1, 128]], channel_multiplier=1).then_inc(identities, 1)
            for part in range(PARTS):
                v = sel[32 * part:32 * part + 32, :, :]
                pool.wait_ge(identities, 2 + part)
                pool.affine_select(out=v, in_=v, compare_op=ALU.not_equal, fill=1.0, base=0,
                                   pattern=[[-1, BC], [0, 128]], channel_multiplier=1).then_inc(identities, 1)

            def times_b(n, i):
                if n >= LAST:
                    return
                wait(pool, u_ready, n // NST + 1, 1, i)
                wait(pool, b_copied, n + 1, NST, i)
                wait(pool, summed, n + 1 - SLOTS, NST, i)
                pool.tensor_tensor(tile(n), u[n // NST % 2][:, :, :], over_halves(b_copy[:, n % B_COPIES, :]),
                                   ALU.mult).then_inc(input_ready, 1)

            def times_c(n, i):
                if n < 0 or n % NST not in POOL_C:
                    return
                j = taken(POOL_C, n)
                wait(pool, scanned, 2 * n + 2, 2 * NST, i)
                wait(pool, c_copied, j + 1, len(POOL_C), i)
                pool.tensor_tensor(tile(n), tile(n), over_halves(c_copy[:, c_slot(n), :]),
                                   ALU.mult).then_inc(output_pool, 1)

            def prepare(k, s, i):
                if k >= ITEMS:
                    return
                m = k % 2
                if s == AT_LOW:
                    wait(pool, mid_ready, k + 1, 1, i)
                    pool.tensor_tensor(split[m][0:32, :], split_rest[0:32, :], split[m][0:32, :],
                                       ALU.subtract).then_inc(split_ready, 1)
                if s == AT_LOG1P:
                    wait(pool, lost_ready, k + 1, 1, i)
                    wait(pool, ln_ready, k + 1, 1, i)
                    pool.tensor_tensor(sp_ln[:, :, :], sp_ln[:, :, :], sp_one[:, :, :],
                                       ALU.subtract).then_inc(log1p_ready, 1)

            pool.wait_ge(identities, 2 + PARTS)
            for part in range(PARTS):
                pool.memset(pad[part][:, :, :, :], 0.0).then_inc(pads_zero, 1)
            for s in range(NST):
                prepare(0, s, 0)
            for n in range(LEAD - 1):
                times_b(n, 0)

            def slot(k, s, i):
                n = NST * k + s
                times_b(n + LEAD - 1, i)
                times_c(n - 1, i)
                prepare(k + 1, s, i)

            run_items(pool, slot)
            times_c(LAST - 1, 0)

        @block.scalar
        def _(act):
            def copy(o, i_):
                return act.activation(o, i_, ACT.Copy)

            act.wait_ge(load_w, W_LOADS)
            for m in range(2):
                act.activation(a_neg[m][:, :, :], a_neg[m][:, :, :], ACT.Exp).then_inc(a_exp, 1)
            for g in range(0, NG, 2):
                setup_copy(act, copy, g, setup_act)
            act.wait_ge(load_k, K_LOADS)
            for n in range(2):
                act.activation(k_sign[n][:, :], k_raw[n][:, :], ACT.Sign).then_inc(k_signed, 1)
            for n in range(2):
                act.wait_ge(setup_mm, NG + 2 * n + 1)
                copy(k_t[n][:, 0:8, :].rearrange("p a e -> p (a e)"), sign_bank(n, 0)).then_inc(setup_act, 1)

            def copy_b(n, i):
                if n >= LAST:
                    return
                wait(act, b_ready, n + 1, NST, i)
                wait(act, input_ready, n + 1 - B_COPIES, NST, i)
                copy(b_copy[:, n % B_COPIES, :], b_row[:, :]).then_inc(b_copied, 1)

            def copy_c(n, i):
                if n >= LAST or n % NST not in POOL_C:
                    return
                wait(act, c_ready, n + 1, NST, i)
                wait(act, output_pool, taken(POOL_C, n) + 1 - C_COPIES, len(POOL_C), i)
                copy(c_copy[:, c_slot(n), :], c_row[:, :]).then_inc(c_copied, 1)

            def decays(n, i):
                if n >= LAST:
                    return
                m, s = n // NST % 2, n % NST
                wait(act, dt_ready, n // NST + 1, 1, i)
                for h in range(HALVES):
                    wait(act, scanned, decay_free(n, h), 2 * NST, i)
                    act.activation(decay_bank(n, h)[:, :].rearrange("p (q l) -> p q l", l=L)[:, :, 1:],
                                   dt[m][:, h, :].rearrange("p (q l) -> p q l", l=L)[:, :, 1:],
                                   ACT.Exp, scale=a_neg[m][:, h, s:s + 1]).then_inc(decay_ready, 1)

            def prepare(k, s, i):
                if k >= ITEMS:
                    return
                m = k % 2
                mm = 7 * k
                if s == AT_SILU:
                    wait(act, gated, k - 1, 1, i)
                    for h in range(HALVES):
                        wait(act, pre_mm, mm + 2 + h + 1, 7, i)
                        act.activation(gate[m][:, h, :], work[:, :], ACT.Silu).then_inc(gate_ready, 1)
                        for half in ((0, 1) if h == 0 else ()):
                            wait(act, tap_done, 8 * k + 6 + half + 1, 8, i)
                            act.activation(xc[m][:, half, :], cv[:, half, :], ACT.Silu,
                                           bias=conv_b[m][:, half:half + 1]).then_inc(xc_ready, 1)
                    act.preload_act_table_set("natural_log_exp_and_others")
                if s == AT_DBC:
                    wait(act, pre_mm, mm + 5, 7, i)
                    copy(dt_low[PARTS * 32:, :], work[PARTS * 32:PARTS * 32 + RANK, :]).then_inc(dt_low_ready, 1)
                    wait(act, c_ready, NST * (k - 1), NST, i)
                    copy(split[m][:, :], work[0:PARTS * 32, :]).then_inc(hi_ready, 1)
                if s == AT_MID:
                    wait(act, rest_ready, k + 1, 1, i)
                    copy(split[m][0:64, :], split_rest[:, :]).then_inc(mid_ready, 1)
                if s in (AT_DT, AT_DT + 1):
                    h = s - AT_DT
                    wait(act, pre_mm, mm + 5 + h + 1, 7, i)
                    if h == 0:
                        wait(act, dt_ready, k, 1, i)
                    src = work
                    act.activation(sp_e[:, h, :], src[:, :], ACT.Abs, bias=b_dt[m][:, h:h + 1]).then_inc(abs_ready, 1)
                    act.activation(sp_relu[:, h, :], src[:, :], ACT.Relu,
                                   bias=b_dt[m][:, h:h + 1]).then_inc(relu_ready, 1)
                if s == AT_EXP:
                    wait(act, abs_ready, 2 * k + 2, 2, i)
                    act.activation(sp_e[:, :, :], sp_e[:, :, :], ACT.Exp, scale=-1.0).then_inc(exp_ready, 1)
                if s == AT_LN:
                    wait(act, exp_ready, k + 1, 1, i)
                    act.activation(sp_one[:, :, :], sp_e[:, :, :], ACT.Identity, bias=1.0).then_inc(one_ready, 1)
                    act.activation(sp_ln[:, :, :], sp_e[:, :, :], ACT.Ln, bias=1.0).then_inc(ln_ready, 1)

            def pad_projected(k, h, i):
                if k >= ITEMS:
                    return
                wait(act, pre_mm, 7 * k + h + 1, 7, i)
                wait(act, tap_done, 8 * k, 8, i)
                act.activation(xpad[:, h, :, LPAD:], work[:, :].rearrange("p (q l) -> p q l", l=L),
                               ACT.Copy).then_inc(xpad_ready, 1)

            for h in range(HALVES):
                pad_projected(0, h, 0)
            for s in range(NST):
                prepare(0, s, 0)
            for h in range(HALVES):
                pad_projected(1, h, 0)
            for n in range(LEAD):
                copy_b(n, 0)
            act.wait_ge(a_ready, 2)
            act.wait_ge(zeros, 4 + DECAYS)
            decays(0, 0)

            def slot(k, s, i):
                n = NST * k + s
                copy_b(n + LEAD, i)
                copy_c(n, i)
                decays(n + 1, i)
                prepare(k + 1, s, i)
                if s >= AT_PROJ:
                    pad_projected(k + 2, s - AT_PROJ, i)

            run_items(act, slot)

            for layer in range(2):
                act.wait_ge(bn_mv, layer + 1)
                if layer == 0:
                    act.activation(bn_tmp[:, 0:1], mv[:, 1:2], ACT.Sqrt, bias=eps[:, 0:1]).then_inc(bn_std, 1)
                else:
                    act.activation(bn_tmp[:, 0:1], mv[:, 1:2], ACT.Sqrt, bias=eps[:, 0:1],
                                   scale=k_mean_sq[:, 0:1]).then_inc(bn_std, 1)
                act.wait_ge(bn_ready, layer + 1)
                for n in range(TILES):
                    b, half = n // 2, n % 2
                    src = (res[:, b, half * CHUNK:(half + 1) * CHUNK] if layer == 0 else bank[n][:, :])
                    src3 = src.rearrange("p (r w) -> p r w", w=W)
                    if layer == 0 and n == 0:
                        act.wait_ge(pads_zero, PARTS)
                    act.activation(inner(0, n), src3, ACT.Relu, bias=bn_b[layer][:, 0:1],
                                   scale=bn_a[layer][:, 0:1]).then_inc(act_hi, 1)
                    g = TILES * layer + n
                    if g >= 2:
                        act.wait_ge(act_rest, g - 1)
                    act.activation(act_f[:, n % 2, :], src, ACT.Relu, bias=bn_b[layer][:, 0:1],
                                   scale=bn_a[layer][:, 0:1]).then_inc(act_full, 1)

        @block.vector
        def _(dve):
            for m in range(2):
                dve.memset(w_dt_raw[m][:, :, 0:PARTS * 32], 0.0).then_inc(zeros, 1)
            dve.memset(xpad[:, :, :, 0:LPAD], 0.0).then_inc(zeros, 1)
            for h in range(DECAYS):
                dve.memset(decay[h][:, :].rearrange("p (q l) -> p q l", l=L)[:, :, 0:1], 0.0).then_inc(zeros, 1)
            dve.memset(eps[:, :], EPS).then_inc(zeros, 1)
            for m in range(2):
                dve.wait_ge(a_exp, m + 1)
                dve.tensor_scalar(a_neg[m][:, :, :], a_neg[m][:, :, :], -1.0, None, ALU.mult).then_inc(a_ready, 1)
            for g in range(1, NG, 2):
                setup_copy(dve, dve.tensor_copy, g, setup_dve)
            dve.wait_ge(load_k, K_LOADS)
            for n in range(2):
                dve.tensor_reduce(k_abs[:, n:n + 1], k_raw[n][:, :], AX.X, ALU.add,
                                  apply_absolute_value=True).then_inc(k_summed, 1)
            for n in range(2):
                dve.wait_ge(setup_mm, NG + 2 * n + 2)
                dve.tensor_copy(k_t[n][:, 8, :], sign_bank(n, 1)[:, 0:128]).then_inc(setup_dve, 1)
            dve.wait_ge(k_mean_mm, 1)
            dve.tensor_scalar(k_mean[:, :], b_row[:, 0:2], 1.0 / WCOUNT, None, ALU.mult).then_inc(k_mean_ready, 1)
            dve.wait_ge(k_mean_ready, 1)
            dve.tensor_tensor(k_mean_sq[:, :], k_mean[:, :], k_mean[:, :], ALU.mult).then_inc(k_mean_ready, 1)

            def scan(n, i):
                wait(dve, input_ready, n + 1, NST, i)
                for h in range(HALVES):
                    wait(dve, decay_ready, 2 * n + h + 1, 2 * NST, i)
                    dve.tensor_tensor_scan(tile(n)[:, h, :], decay_bank(n, h)[:, :], tile(n)[:, h, :], 0.0,
                                           ALU.mult, ALU.add).then_inc(scanned, 1)

            def times_c(n, i):
                if n < 0 or n % NST in POOL_C:
                    return
                wait(dve, scanned, 2 * n + 2, 2 * NST, i)
                wait(dve, c_ready, n + 1, NST, i)
                dve.tensor_tensor(tile(n), tile(n), over_halves(c_row[:, :]), ALU.mult).then_inc(output_dve, 1)

            def prepare(k, s, i):
                if k >= ITEMS:
                    return
                m = k % 2
                if s in AT_TAPS:
                    tap = AT_TAPS.index(s)
                    for h in range(HALVES):
                        src = xpad[:, h, :, tap:tap + L]
                        acc = cv[:, h, :].rearrange("p (q l) -> p q l", l=L)
                        w = conv_w[m][:, h, tap:tap + 1]
                        if tap == 0:
                            wait(dve, xpad_ready, 2 * k + h + 1, 2, i)
                            wait(dve, xc_ready, 2 * k, 2, i)
                            dve.tensor_scalar(acc, src, w, None, ALU.mult).then_inc(tap_done, 1)
                        else:
                            wait(dve, tap_done, 8 * k + 2 * (tap - 1) + h + 1, 8, i)
                            dve.scalar_tensor_tensor(acc, src, w, acc, ALU.mult, ALU.add).then_inc(tap_done, 1)
                if s == AT_REST:
                    wait(dve, hi_ready, k + 1, 1, i)
                    wait(dve, split_ready, k, 1, i)
                    dve.tensor_tensor(split_rest[:, :], work[0:64, :], split[m][0:64, :],
                                      ALU.subtract).then_inc(rest_ready, 1)
                if s == AT_LOST:
                    wait(dve, one_ready, k + 1, 1, i)
                    dve.scalar_tensor_tensor(sp_one[:, :, :], sp_one[:, :, :], 1.0, sp_e[:, :, :],
                                             ALU.subtract, ALU.subtract).then_inc(lost_ready, 1)
                if s == AT_U:
                    wait(dve, log1p_ready, k + 1, 1, i)
                    wait(dve, relu_ready, 2 * k + 2, 2, i)
                    wait(dve, decay_ready, 2 * NST * (k - 1), 2 * NST, i)
                    dve.tensor_tensor(dt[m][:, :, :], sp_ln[:, :, :], sp_relu[:, :, :], ALU.add).then_inc(dt_ready, 1)
                    wait(dve, dt_ready, k + 1, 1, i)
                    wait(dve, xc_ready, 2 * k + 2, 2, i)
                    wait(dve, scanned, 2 * NST * (k - 1), 2 * NST, i)
                    dve.tensor_tensor(u[m][:, :, :], dt[m][:, :, :], xc[m][:, :, :], ALU.mult).then_inc(u_ready, 1)

            def post(k, i):
                m, j = k % 2, k // 2 % 2
                wait(dve, summed, NST * (k + 1), NST, i)
                for h in range(HALVES):
                    dve.scalar_tensor_tensor(xc[m][:, h, :], xc[m][:, h, :], d_skip[m][:, h:h + 1],
                                             y_sum[h][:, :], ALU.mult, ALU.add).then_inc(y_read, 1)
                wait(dve, y_read, 2 * k + 2, 2, i)
                wait(dve, gate_ready, 2 * k + 2, 2, i)
                dve.tensor_tensor(y_gated[:, 2 * m:2 * m + 2, j * CHUNK:(j + 1) * CHUNK], xc[m][:, :, :],
                                  gate[m][:, :, :], ALU.mult).then_inc(gated, 1)

            def add_output(k, part, i):
                b = k // ITEMS_PER_IMAGE - 1 + i
                wait_image(dve, out_mm, 2 * (k // ITEMS_PER_IMAGE - 1) + part + 1, i)
                dst = res[:, bass.ds(b, 1), part * CHUNK:(part + 1) * CHUNK].rearrange("p b n -> p (b n)")
                dve.tensor_tensor(dst, dst, work[:, :], ALU.add).then_inc(res_added, 1)

            for s in range(NST):
                prepare(0, s, 0)
            dve.wait_ge(load_res, 16 * NB)

            def slot(k, s, i):
                n = NST * k + s
                scan(n, i)
                times_c(n - 1, i)
                if s == AT_POST and k > 0:
                    post(k - 1, i)
                if k % ITEMS_PER_IMAGE == 0 and k > 0 and s in (AT_OUT + 1, AT_OUT + 3):
                    add_output(k, (s - AT_OUT) // 2, i)
                prepare(k + 1, s, i)

            run_items(dve, slot)
            times_c(LAST - 1, 0)
            post(ITEMS - 1, 0)
            for part in range(2):
                add_output(ITEMS, part, 0)

            for layer in range(2):
                for n in range(TILES):
                    b, half = n // 2, n % 2
                    if layer == 0:
                        if n == 0:
                            dve.wait_ge(res_added, 2 * NB)
                        src = res[:, b, half * CHUNK:(half + 1) * CHUNK]
                    else:
                        dve.wait_ge(conv_mm, n + 1)
                        src = bank[n][:, :]
                    dve.bn_stats(stats[:, n, :], src).then_inc(stat_done, 1)
                dve.wait_ge(stat_done, TILES * (layer + 1))
                dve.bn_aggr(mv[:, :], stats[:, :, :].rearrange("p a b -> p (a b)")).then_inc(bn_mv, 1)
                dve.wait_ge(bn_std, layer + 1)
                q = 3 * layer
                dve.reciprocal(bn_tmp[:, 1:2], bn_tmp[:, 0:1]).then_inc(bn_step, 1)
                dve.wait_ge(bn_step, q + 1)
                if layer == 0:
                    dve.tensor_tensor(bn_a[0][:, :], bn_tmp[:, 1:2], gamma[0][:, :], ALU.mult).then_inc(bn_step, 1)
                else:
                    dve.scalar_tensor_tensor(bn_a[1][:, :], bn_tmp[:, 1:2], k_mean[:, 0:1], gamma[1][:, :],
                                             ALU.mult, ALU.mult).then_inc(bn_step, 1)
                dve.wait_ge(bn_step, q + 2)
                dve.wait_ge(bn_mv, layer + 1)
                dve.tensor_tensor(bn_tmp[:, 2:3], mv[:, 0:1], bn_a[layer][:, :], ALU.mult).then_inc(bn_step, 1)
                dve.wait_ge(bn_step, q + 3)
                dve.tensor_tensor(bn_b[layer][:, :], beta[layer][:, :], bn_tmp[:, 2:3],
                                  ALU.subtract).then_inc(bn_ready, 1)
                for n in range(TILES):
                    g = TILES * layer + n
                    rest = act_r[:, n % 2, :].rearrange("p (r w) -> p r w", w=W)
                    full = act_f[:, n % 2, :].rearrange("p (r w) -> p r w", w=W)
                    dve.wait_ge(act_full, g + 1)
                    dve.wait_ge(act_hi, g + 1)
                    if g >= 2:
                        dve.wait_ge(act_lo, g - 1)
                    dve.tensor_tensor(rest, full, inner(0, n), ALU.subtract).then_inc(act_rest, 1)
                    dve.wait_ge(act_rest, g + 1)
                    dve.tensor_copy(inner(1, n), rest).then_inc(act_mid, 1)
                    dve.wait_ge(act_mid, g + 1)
                    dve.tensor_tensor(inner(2, n), rest, inner(1, n), ALU.subtract).then_inc(act_lo, 1)
            for n in range(TILES):
                b, half = n // 2, n % 2
                dst = res[:, b, half * CHUNK:(half + 1) * CHUNK]
                dve.wait_ge(conv_mm, TILES + n + 1)
                dve.scalar_tensor_tensor(dst, bank[n][:, :], k_mean[:, 1:2], dst,
                                         ALU.mult, ALU.add).then_inc(y_ready, 1)

        @block.tensor
        def _(pe):
            pe.wait_ge(identities, 2 + PARTS)
            pe.wait_ge(consts, 4)
            pe.wait_ge(zeros, 2)
            pe.wait_ge(load_w, W_LOADS)
            groups_x = 0
            for g, (kind, parts, _, _, _, _) in enumerate(GROUPS):
                if g >= 4:
                    if g % 2 == 0:
                        pe.wait_ge(setup_act, (g - 4) // 2 + 1)
                    else:
                        pe.wait_ge(setup_dve, (g - 4) // 2 + 1)
                if kind == "x":
                    pe.wait_ge(load_x, 16 * (groups_x // 2 + 1))
                    groups_x += 1
                for src, cols, at in parts:
                    rows = src.shape[0]
                    b = bank[SETUP_BANKS[g % 4]]
                    mm = pe.transpose(b[0:src.shape[1], at:at + rows], src, ident[0:rows, 0:rows])
                mm.then_inc(setup_mm, 1)
            pe.wait_ge(k_signed, 2)
            pe.wait_ge(setup_act, NG // 2)
            pe.wait_ge(setup_dve, NG // 2)
            for n in range(2):
                taps = k_sign[n][:, :].rearrange("p (i q) -> p q i", q=TAPS)
                for q in range(8):
                    mm = pe.transpose(sign_bank(n, 0)[:, 128 * q:128 * q + 128], taps[:, q, :], ident16[:, :])
                mm.then_inc(setup_mm, 1)
                pe.transpose(sign_bank(n, 1)[:, 0:128], taps[:, 8, :], ident16[:, :]).then_inc(setup_mm, 1)
            pe.wait_ge(k_summed, 2)
            pe.matmul(b_row[:, 0:2], ones[:, :], k_abs[:, :]).then_inc(k_mean_mm, 1)

            def spread(row, n, ready, i):
                wait(pe, split_ready, n // NST + 1, 1, i)
                target = b_row if row < NST else c_row
                pe.matmul(target[:, :], sel[:, row, :], split[n // NST % 2][:, :]).then_inc(ready, 1)

            def spread_b(n, i):
                if n >= LAST:
                    return
                wait(pe, b_copied, n, NST, i)
                spread(n % NST, n, b_ready, i)

            def spread_c(n, i):
                if (n - 1) % NST in POOL_C:
                    wait(pe, c_copied, taken(POOL_C, n), len(POOL_C), i)
                elif n > 0:
                    wait(pe, output_dve, n - taken(POOL_C, n), NST - len(POOL_C), i)
                spread(NST + n % NST, n, c_ready, i)

            def sum_states(n, i):
                if n < 0:
                    return
                wait_output(pe, n, i)
                if n % NST == 0:
                    wait(pe, y_read, 2 * (n // NST), 2, i)
                for h in range(HALVES):
                    mm = pe.matmul(y_sum[h][:, :], ident[:, :], tile(n)[:, h, :],
                                   start=(n % NST == 0), stop=(n % NST == NST - 1))
                mm.then_inc(summed, 1)

            def prepare(k, s, i):
                if k >= ITEMS:
                    return
                m = k % 2
                if s in (AT_GATE, AT_GATE + 1):
                    h = s - AT_GATE
                    if h == 0:
                        wait(pe, xpad_ready, 2 * k + 2, 2, i)
                    else:
                        wait(pe, gate_ready, 2 * k + 1, 2, i)
                    pe.matmul(work[:, :], w_in[m][:, HALVES + h, :], chunk_of(k, i)).then_inc(pre_mm, 1)
                if s == AT_DBC:
                    wait(pe, gate_ready, 2 * k + 2, 2, i)
                    wait(pe, xc_ready, 2 * k + 2, 2, i)
                    for h in range(HALVES):
                        mm = pe.matmul(work[0:PARTS * 32 + RANK, :], w_x[m][:, h, :], xc[m][:, h, :],
                                       start=(h == 0), stop=(h == HALVES - 1))
                    mm.then_inc(pre_mm, 1)
                if s in (AT_DT, AT_DT + 1):
                    h = s - AT_DT
                    if h == 0:
                        wait(pe, dt_low_ready, k + 1, 1, i)
                        wait(pe, rest_ready, k + 1, 1, i)
                    else:
                        wait(pe, relu_ready, 2 * k + 1, 2, i)
                    pe.matmul(work[:, :], w_dt[m][PARTS * 32:, 128 * h:128 * h + 128],
                              dt_low[PARTS * 32:, :]).then_inc(pre_mm, 1)

            def chunk_of(k, i):
                return x_t[:, bass.ds(k // 2 * CHUNK + i * (2 * CHUNK), CHUNK)]

            def project(k, h, i):
                if k >= ITEMS:
                    return
                if h == 0:
                    wait(pe, relu_ready, 2 * k, 2, i)
                else:
                    wait(pe, xpad_ready, 2 * k + 1, 2, i)
                pe.matmul(work[:, :], w_in[k % 2][:, h, :], chunk_of(k, i)).then_inc(pre_mm, 1)

            def project_out(k, r, i):
                q = r % 4
                if r == 0:
                    wait(pe, gated, k, 1, i)
                    if k < ITEMS:
                        wait(pe, relu_ready, 2 * (k + 1) + 2, 2, i)
                if r == 4:
                    wait_image(pe, res_added, 2 * (k // ITEMS_PER_IMAGE) - 1, i)
                for g in range(4):
                    mm = pe.matmul(work[:, 128 * q:128 * q + 128],
                                   y_gated[:, g, r:HW:8], w_out[g // 2][:, g % 2, :],
                                   start=(g == 0), stop=(g == 3), skip_group_check=True)
                if q == 3:
                    mm.then_inc(out_mm, 1)

            pe.wait_ge(k_mean_ready, 1)
            pe.wait_ge(setup_act, NG // 2 + 2)
            pe.wait_ge(setup_dve, NG // 2 + 2)
            for h in range(HALVES):
                project(0, h, 0)
            for s in range(NST):
                prepare(0, s, 0)
            for h in range(HALVES):
                project(1, h, 0)
            for n in range(LEAD):
                spread_b(n, 0)

            def slot(k, s, i):
                n = NST * k + s
                spread_b(n + LEAD, i)
                sum_states(n - LAG, i)
                spread_c(n, i)
                prepare(k + 1, s, i)
                if k % ITEMS_PER_IMAGE == 0 and k > 0:
                    if AT_OUT <= s < AT_OUT + 4:
                        project_out(k, 2 * (s - AT_OUT), i)
                        project_out(k, 2 * (s - AT_OUT) + 1, i)
                    if s == AT_OUT + 4:
                        wait_image(pe, res_added, 2 * (k // ITEMS_PER_IMAGE), i)
                if s >= AT_PROJ:
                    project(k + 2, s - AT_PROJ, i)

            run_items(pe, slot)
            for n in range(LAST - LAG, LAST):
                sum_states(n, 0)
            for r in range(8):
                project_out(ITEMS, r, 0)

            for layer in range(2):
                for n in range(TILES):
                    b, r = n // 2, ROWS * (n % 2)
                    if n % 2 == 0:
                        pe.wait_ge(act_lo, TILES * layer + n + 2)
                    for q in range(TAPS):
                        for part in range(PARTS):
                            src = pad[part][:, b, r + q // 3:r + q // 3 + ROWS, q % 3:q % 3 + W]
                            mm = pe.matmul(bank[n][:, :].rearrange("p (r w) -> p r w", w=W), k_t[layer][:, q, :], src,
                                           start=(q == 0 and part == 0), stop=(q == TAPS - 1 and part == PARTS - 1))
                    mm.then_inc(conv_mm, 1)


_INS = ['x'] + [f'L0_conv_{n}{m}' for m in (1, 2) for n in
                ('W_in', 'conv_w', 'conv_b', 'W_x', 'W_dt', 'b_dt', 'A_log', 'D_skip', 'W_out')] + \
       [f'L1_conv_{n}' for n in ('gamma0', 'beta0', 'w0', 'gamma1', 'beta1', 'w1')]


def kernel(**inputs):
    import numpy as _np
    import concourse.bacc as _bacc
    from concourse import mybir as _mybir
    from concourse.bass_utils import run_bass_kernel_spmd as _run

    nc = _bacc.Bacc("TRN2", target_bir_lowering=False, num_devices=1)
    arrays, tensors = {}, {}
    for name in _INS:
        a = _np.ascontiguousarray(inputs[name])
        arrays[f"in_{name}_dram"] = a
        tensors[name] = nc.dram_tensor(f"in_{name}_dram", a.shape, _mybir.dt.from_np(a.dtype),
                                       kind="ExternalInput").ap()
    out = nc.dram_tensor("out_0_dram", (NB, C, H, W), F32, kind="ExternalOutput").ap()
    mamba_conv_kernel(nc, tensors, out)
    r = _run(nc, [arrays], core_ids=[0])
    return r.results[0]["out_0_dram"]
```

```python
from contextlib import ExitStack

import concourse.bass as bass
from concourse import mybir

ALU = mybir.AluOpType
ACT = mybir.ActivationFunctionType
AX = mybir.AxisListType
F32 = mybir.dt.float32
BF16 = mybir.dt.bfloat16

NB, C, H, W = 4, 128, 32, 32
HW = H * W
D = C
L = W
E_IN = 2 * D
HALVES = E_IN // 128
NST = 16
RANK = D // 16
VECTORS = 3
KCONV = 4
TOKENS = NB * HW
CHUNK = 512
CSEQ = CHUNK // L
MAMBAS = 2
CHUNKS_PER_IMAGE = HW // CHUNK
ITEMS_PER_IMAGE = CHUNKS_PER_IMAGE * MAMBAS
ITEMS = NB * ITEMS_PER_IMAGE
BC = 2 * NST
PARTS = 3
LPAD = KCONV - 1
TAPS = 9
EPS = 1e-5
HP, WP = H + 2, W + 2
TILES = NB * 2
ROWS = H // 2
WCOUNT = C * C * TAPS

SLOTS = 8
LAG = 3
POOL_LEAD = 3
CATCH_UP = 6
LEAD = 5
B_COPIES, C_COPIES = 4, 2
DECAYS = 3
SPARES = (7,)

POOL_C = (2, 9, 12)

AT_PROJ = (9, 9, 10, 11, 12, 13, 14, 15)
AT_PROJ_OUT = (12, 12, 13, 13, 14, 14, 15, 15)
AT_PROJ_FIRST = (9, 9, 10, 10, 11, 12, 13, 14)
AT_X = (11, 16)
AT_X_OUT = (14, 16)
AT_X_FIRST = (11, 15)
AT_POST = LAG
AT_GATE = 3
AT_Z = 4
AT_SILU = 5
AT_DBC = 6
AT_HIGH = 6
AT_REST = 8
AT_MID = 8
AT_LOW = 9
AT_DT = 7
AT_EXP = 9
AT_LN = 10
AT_LOST = 11
AT_LOG1P = 11
AT_U = 12
AT_EARLY = 9
AT_KERNELS = (9, 10, 11)
AT_STATS = 8
AT_OUT = (9, 0)


def mamba_conv_kernel(nc, t, out):
    x = t["x"]
    ctx = ExitStack()
    with ctx:
        def sb(name, shape, dt=F32):
            return ctx.enter_context(nc.sbuf_tensor(name, shape, dt))

        def sem(name):
            return ctx.enter_context(nc.semaphore(name))

        ident = sb("ident", [128, 128])
        ident16 = sb("ident16", [128, 128], BF16)
        ones = sb("ones", [128, 128])
        sel = sb("sel", [PARTS * 32, BC, 128], BF16)
        eps = sb("eps", [128, 1])
        state = sb("state", [128, SLOTS, HALVES, CHUNK])
        raw = state[:, :, :, :].rearrange("p a h n -> p (a h n)")
        raw_used = [0]

        def staged(columns):
            raw_used[0] += columns
            assert raw_used[0] <= SLOTS * HALVES * CHUNK
            return raw[:, raw_used[0] - columns:raw_used[0]]

        XROWS = PARTS * 32 + RANK
        w_in_raw = [staged(4 * 128).rearrange("p (a d) -> p a d", a=4) for m in range(2)]
        w_x_raw = [staged(E_IN)[0:XROWS, :] for m in range(2)]
        w_dt_raw = [staged(HALVES * XROWS).rearrange("p (a r) -> p a r", a=HALVES) for m in range(2)]
        w_out_raw = [staged(E_IN) for m in range(2)]
        vectors_raw = [staged(128)[0:VECTORS * HALVES, :] for m in range(2)]
        w_tap_raw = [staged(HALVES * KCONV * 128).rearrange("p (h k d) -> p h k d", h=HALVES, k=KCONV)
                     for m in range(2)]
        w_tap = [sb(f"w_tap{m}", [128, HALVES, KCONV, 128]) for m in range(2)]
        w_z = [sb(f"w_z{m}", [128, HALVES, 128]) for m in range(2)]
        w_x = [sb(f"w_x{m}", [128, HALVES, PARTS * 32 + RANK]) for m in range(2)]
        w_dt = [sb(f"w_dt{m}", [PARTS * 32 + RANK, E_IN]) for m in range(2)]
        w_out = [sb(f"w_out{m}", [128, HALVES, 128]) for m in range(2)]
        conv_w = [sb(f"conv_w{m}", [128, HALVES, KCONV]) for m in range(2)]
        vectors = [sb(f"vectors{m}", [128, VECTORS * HALVES]) for m in range(2)]
        conv_b, b_dt, d_skip = ([vectors[m][:, HALVES * v:HALVES * v + HALVES] for m in range(2)]
                                for v in range(VECTORS))
        a_neg = [sb(f"a_neg{m}", [128, HALVES, NST]) for m in range(2)]
        k_t = [sb(f"k_t{n}", [128, TAPS, 128], BF16) for n in range(2)]
        k_abs = sb("k_abs", [128, 2])
        k_mean = sb("k_mean", [128, 2])
        k_mean_sq = sb("k_mean_sq", [128, 2])
        gamma = [sb(f"gamma{n}", [128, 1]) for n in range(2)]
        beta = [sb(f"beta{n}", [128, 1]) for n in range(2)]

        x_tok = sb("x_tok", [128, TOKENS // 128, 128])
        y_gated = x_tok[:, :, :].rearrange("p a d -> p (a d)").rearrange("p (g n) -> p g n", g=4)
        tok = x_tok[:, :, :].rearrange("p a d -> p (a d)")
        k_raw = [tok[:, n * C * TAPS:(n + 1) * C * TAPS] for n in range(2)]
        k_sign = [tok[:, (4 + n) * C * TAPS // 2:(5 + n) * C * TAPS // 2].bitcast(BF16) for n in range(2)]
        x_t = sb("x_t", [128, TOKENS // L, LPAD + L])
        res = sb("res", [128, NB, HW])
        cv = sb("cv", [128, HALVES, CHUNK])
        xc = [sb(f"xc{m}", [128, HALVES, CHUNK]) for m in range(2)]
        gate = [sb(f"gate{m}", [128, HALVES, CHUNK]) for m in range(2)]
        dt = [sb(f"dt{m}", [128, HALVES, CHUNK]) for m in range(2)]
        u = [sb(f"u{m}", [128, HALVES, CHUNK]) for m in range(2)]
        split = [sb(f"split{m}", [PARTS * 32, CHUNK], BF16) for m in range(2)]
        split_rest = sb("split_rest", [64, CHUNK])
        dbc = sb("dbc", [PARTS * 32 + RANK, CHUNK])
        sp_e = sb("sp_e", [128, HALVES, CHUNK])
        sp_ln = sb("sp_ln", [128, HALVES, CHUNK])
        sp_one = sb("sp_one", [128, HALVES, CHUNK])
        b_copy = sb("b_copy", [128, B_COPIES, CHUNK])
        c_copy = sb("c_copy", [128, C_COPIES, CHUNK])
        pad = [sb(f"pad{p}", [128, NB, HP, WP], BF16) for p in range(PARTS)]
        SPARE_PADS = range(PARTS - len(SPARES), PARTS)
        spare = [pad[p][:, :, :, :].rearrange("p b h w -> p (b h w)")[:, 0:2 * HALVES * CHUNK].bitcast(
            F32).rearrange("p (h n) -> p h n", h=HALVES) for p in SPARE_PADS]
        act_f, act_r = b_copy[:, 0:2, :], b_copy[:, 2:4, :]
        stats = sb("stats", [128, TILES, 6])
        mv = sb("mv", [128, 2])
        bn_tmp = sb("bn_tmp", [128, 4])
        bn_a = [sb(f"bn_a{n}", [128, 1]) for n in range(2)]
        bn_b = [sb(f"bn_b{n}", [128, 1]) for n in range(2)]

        bank = [ctx.enter_context(nc.psum_tensor(f"bank{i}", [128, CHUNK], F32)) for i in range(8)]
        decay = bank[0:DECAYS]
        b_row, c_row = bank[3], bank[4]
        y_sum = bank[5:7]
        work = bank[7]

        load_w = [sem(f"load_w{m}") for m in range(2)]
        load_x = sem("load_x")
        load_res = sem("load_res")
        load_k = sem("load_k")
        consts = sem("consts")
        zeros = sem("zeros")
        pads_zero = sem("pads_zero")
        identities = sem("identities")
        a_exp = sem("a_exp")
        a_ready = sem("a_ready")
        taps_ready = sem("taps_ready")
        k_signed = sem("k_signed")
        k_mm = sem("k_mm")
        k_copied = sem("k_copied")
        k_summed = sem("k_summed")
        k_mean_ready = sem("k_mean_ready")
        setup_mm = sem("setup_mm")
        setup_act = sem("setup_act")
        setup_dve = sem("setup_dve")
        pre_mm = sem("pre_mm")
        cv_ready = sem("cv_ready")
        z_ready = sem("z_ready")
        xc_ready = sem("xc_ready")
        gate_ready = sem("gate_ready")
        dbc_ready = sem("dbc_ready")
        hi_ready = sem("hi_ready")
        rest_ready = sem("rest_ready")
        mid_ready = sem("mid_ready")
        split_ready = sem("split_ready")
        abs_ready = sem("abs_ready")
        relu_ready = sem("relu_ready")
        exp_ready = sem("exp_ready")
        ln_ready = sem("ln_ready")
        one_ready = sem("one_ready")
        lost_ready = sem("lost_ready")
        log1p_ready = sem("log1p_ready")
        dt_ready = sem("dt_ready")
        u_ready = sem("u_ready")
        b_ready = sem("b_ready")
        c_ready = sem("c_ready")
        b_copied = sem("b_copied")
        c_copied = sem("c_copied")
        decay_ready = sem("decay_ready")
        input_ready = sem("input_ready")
        scanned = sem("scanned")
        output_dve = sem("output_dve")
        output_pool = sem("output_pool")
        summed = sem("summed")
        y_read = sem("y_read")
        gated = sem("gated")
        out_mm = sem("out_mm")
        res_added = sem("res_added")
        stat_done = sem("stat_done")
        bn_mv = sem("bn_mv")
        bn_std = sem("bn_std")
        bn_step = sem("bn_step")
        bn_ready = sem("bn_ready")
        act_hi = sem("act_hi")
        act_full = sem("act_full")
        act_rest = sem("act_rest")
        act_mid = sem("act_mid")
        act_lo = sem("act_lo")
        conv_mm = sem("conv_mm")
        y_ready = sem("y_ready")
        y_stored = sem("y_stored")

        block = ctx.enter_context(nc.Block())

        def wait(eng, semaphore, count, per_item, i):
            if count > 0:
                eng.wait_ge(semaphore, count + i * (per_item * ITEMS_PER_IMAGE))

        def wait_image(eng, semaphore, count, i):
            if count > 0:
                eng.wait_ge(semaphore, count + i * 2)

        def taken(states, n):
            return n // NST * len(states) + sum(s < n % NST for s in states)

        def run_items(eng, slot):
            for k in range(PEELED):
                for s in range(NST):
                    slot(k, s, 0)
            with eng.Fori(0, NB - 1) as i:
                for k in range(PEELED, PEELED + ITEMS_PER_IMAGE):
                    for s in range(NST):
                        slot(k, s, i)
            for k in range(ITEMS - ITEMS_PER_IMAGE + PEELED, ITEMS):
                for s in range(NST):
                    slot(k, s, 0)

        LAST = ITEMS * NST
        PEELED = 2

        def out_half(k, s, slots, first=0):
            half = k % ITEMS_PER_IMAGE
            if k >= ITEMS_PER_IMAGE and half < 2 and first <= s - AT_OUT[half] < first + slots:
                return half, s - AT_OUT[half] - first
            return None

        def wait_output(eng, n, i):
            if n % NST in POOL_C:
                wait(eng, output_pool, taken(POOL_C, n) + 1, len(POOL_C), i)
            else:
                wait(eng, output_dve, n - taken(POOL_C, n) + 1, NST - len(POOL_C), i)

        def c_slot(n):
            return taken(POOL_C, n) % C_COPIES

        RING = [(st, h) for st in range(NST) for h in range(HALVES) if st not in SPARES]

        def decay_place(n, h):
            if n % NST in SPARES:
                return spare[SPARES.index(n % NST)][:, h, :]
            return decay[RING.index((n % NST, h)) % DECAYS][:, :]

        def decay_free(n, h):
            before, here = HALVES * NST * (n // NST), (n % NST, h)
            if n % NST in SPARES:
                return before - HALVES * NST + HALVES * (n % NST) + h + 1
            j = RING.index(here)
            if j >= DECAYS:
                st, h = RING[j - DECAYS]
            else:
                st, h = RING[max(q for q in range(len(RING)) if q % DECAYS == j)]
                before -= HALVES * NST
            return before + HALVES * st + h + 1

        def projected(k, half):
            return b_row if k == ITEMS and half == 1 else work

        def due(k, s, usual, with_output):
            for item in (k - 1, k):
                slots = with_output if item % ITEMS_PER_IMAGE == 0 else usual
                for part, at in enumerate(slots):
                    if item >= 0 and at == s + NST * (k - item):
                        yield item, part

        def inner(part, n):
            b, r = n // 2, ROWS * (n % 2)
            return pad[part][:, b, 1 + r:1 + r + ROWS, 1:1 + W]

        def tile(n):
            return state[:, n % SLOTS, :, :]

        def over_halves(row):
            return row.unsqueeze(1).to_broadcast([128, HALVES, CHUNK])

        def load_x_tokens(eng, first, last):
            rows = x.rearrange("b c h w -> (b c h w)").rearrange("(a p d) -> p a d", p=128, d=D)
            a, b = first * CHUNK // 128, last * CHUNK // 128
            eng.dma_start(x_tok[:, a:b, :], rows[:, a:b, :]).then_inc(load_x, 16)

        def load_matrices(eng, m):
            s, w = str(m + 1), t[f"L0_conv_W_x{m + 1}"]
            eng.dma_start(w_in_raw[m][:, :, :],
                          t[f"L0_conv_W_in{s}"].rearrange("(a p) d -> p a d", p=128)).then_inc(load_w[m], 16)
            for part in range(PARTS):
                eng.dma_start(w_x_raw[m][32 * part:32 * part + 32, :], w[RANK:RANK + BC, :]).then_inc(load_w[m], 16)
            eng.dma_start(w_x_raw[m][PARTS * 32:PARTS * 32 + RANK, :], w[0:RANK, :]).then_inc(load_w[m], 16)
            eng.dma_start(w_out_raw[m][:, :], t[f"L0_conv_W_out{s}"]).then_inc(load_w[m], 16)

        def load_vectors(eng, m):
            s = str(m + 1)
            eng.dma_start(conv_w[m][:, :, :],
                          t[f"L0_conv_conv_w{s}"].rearrange("(a p) k -> p a k", p=128)).then_inc(load_w[m], 16)
            eng.dma_start(a_neg[m][:, :, :],
                          t[f"L0_conv_A_log{s}"].rearrange("(a p) n -> p a n", p=128)).then_inc(load_w[m], 16)
            for v, name in enumerate(("conv_b", "b_dt", "D_skip")):
                eng.dma_start(vectors_raw[m][HALVES * v:HALVES * v + HALVES, :],
                              t[f"L0_conv_{name}{s}"].rearrange("(a p) -> a p", p=128)).then_inc(load_w[m], 16)
            eng.wait_ge(zeros, m + 1)
            eng.dma_start(w_dt_raw[m][:, :, PARTS * 32:],
                          t[f"L0_conv_W_dt{s}"].rearrange("(a p) r -> p a r", p=128)).then_inc(load_w[m], 16)

        W_LOADS = 16 * (1 + PARTS + 1 + 1 + 1 + 1 + VECTORS + 1)
        K_LOADS = 16 * 2 * 3

        def weight_groups(m):
            rows = PARTS * 32 + RANK
            for h in range(HALVES):
                yield ("w", m, [w_tap_raw[m][:, h, k, :] for k in range(KCONV)], 128, (0, 128),
                       w_tap[m][:, h, :, :].rearrange("p k e -> p (k e)"))
            yield ("w", m, [w_in_raw[m][:, HALVES + h, :] for h in range(HALVES)], 128, (0, 128),
                   w_z[m][:, :, :].rearrange("p h e -> p (h e)"))
            yield ("w", m, [w_x_raw[m][:, 128 * h:128 * h + 128] for h in range(HALVES)], rows, (0, 128),
                   w_x[m][:, :, :].rearrange("p a e -> p (a e)"))
            yield ("w", m, [w_dt_raw[m][:, h, :] for h in range(HALVES)], 128, (PARTS * 32, rows),
                   w_dt[m][PARTS * 32:, :])
            yield ("w", m, [vectors_raw[m]], VECTORS * HALVES, (0, 128), vectors[m][:, :])
            yield ("w", m, [w_out_raw[m][:, 128 * h:128 * h + 128] for h in range(HALVES)], 128, (0, 128),
                   w_out[m][:, :, :].rearrange("p a e -> p (a e)"))

        def x_group(g):
            return ("x", g, [x_tok[:, 4 * g + a, :] for a in range(4)], 128, (0, 128),
                    x_t[:, g * CSEQ:(g + 1) * CSEQ, LPAD:])

        GROUPS = [*weight_groups(0), x_group(0)]
        FIRST = len(GROUPS)
        GROUPS += [*weight_groups(1), *(x_group(g) for g in range(1, TOKENS // CHUNK))]
        NG = len(GROUPS)
        assert FIRST % 2 == 0 and NG % 2 == 0 and NG - FIRST <= NST
        X_LOADS = [1, 2] + [3] * (TOKENS // CHUNK - 2)

        SETUP_BANKS = 3

        def setup_bank(g):
            return bank[4 + g % SETUP_BANKS]

        def setup_copy(eng, copy, g, done):
            what, _, sources, cols, (lo, hi), target = GROUPS[g]
            src = setup_bank(g)[lo:hi, 0:cols * len(sources)]
            if what == "x":
                src = src.rearrange("p (q l) -> p q l", l=L)
            eng.wait_ge(setup_mm, g + 1)
            copy(target, src).then_inc(done, 1)

        @block.sync
        def _(sp):
            load_matrices(sp, 0)
            load_x_tokens(sp, 1, 2)
            load_matrices(sp, 1)
            load_x_tokens(sp, 2, TOKENS // CHUNK)
            sp.wait_ge(setup_mm, NG)
            for n in range(2):
                sp.dma_start(k_raw[n], t[f"L1_conv_w{n}"].rearrange("o i a b -> o (i a b)")).then_inc(load_k, 16)
                sp.dma_start(gamma[n][:, :], t[f"L1_conv_gamma{n}"].rearrange("(p a) -> p a", a=1)).then_inc(load_k, 16)
                sp.dma_start(beta[n][:, :], t[f"L1_conv_beta{n}"].rearrange("(p a) -> p a", a=1)).then_inc(load_k, 16)
            for b in range(NB):
                sp.dma_start(res[:, b, :], x[b].rearrange("c h w -> c (h w)")).then_inc(load_res, 16)
            for n in range(TILES):
                sp.wait_ge(y_ready, n + 1)
                b, half = n // 2, n % 2
                sp.dma_start(out[b].rearrange("c h w -> c (h w)")[:, half * CHUNK:(half + 1) * CHUNK],
                             res[:, b, half * CHUNK:(half + 1) * CHUNK]).then_inc(y_stored, 16)
            sp.wait_ge(y_stored, 16 * TILES)

        @block.gpsimd
        def _(pool):
            for m in (ident, ident16):
                pool.memset(m[:, :], 0.0).then_inc(consts, 1)
            pool.wait_ge(consts, 2)
            for m in (ident, ident16):
                pool.affine_select(out=m[:, :], in_=m[:, :], compare_op=ALU.not_equal, fill=1.0, base=0,
                                   pattern=[[-1, 128]], channel_multiplier=1).then_inc(identities, 1)
            pool.memset(ones[:, :], 1.0).then_inc(consts, 1)
            pool.memset(sel[:, :, :], 0.0).then_inc(consts, 1)
            for part in range(PARTS):
                v = sel[32 * part:32 * part + 32, :, :]
                pool.wait_ge(consts, 4)
                pool.wait_ge(identities, 2 + part)
                pool.affine_select(out=v, in_=v, compare_op=ALU.not_equal, fill=1.0, base=0,
                                   pattern=[[-1, BC], [0, 128]], channel_multiplier=1).then_inc(identities, 1)

            def times_b(n, i):
                if n >= LAST:
                    return
                wait(pool, u_ready, n // NST + 1, 1, i)
                wait(pool, b_copied, n + 1, NST, i)
                wait(pool, summed, n + 1 - SLOTS, NST, i)
                pool.tensor_tensor(tile(n), u[n // NST % 2][:, :, :], over_halves(b_copy[:, n % B_COPIES, :]),
                                   ALU.mult).then_inc(input_ready, 1)

            def times_c(n, i):
                if n < 0 or n % NST not in POOL_C:
                    return
                j = taken(POOL_C, n)
                wait(pool, scanned, 2 * n + 2, 2 * NST, i)
                wait(pool, c_copied, j + 1, len(POOL_C), i)
                pool.tensor_tensor(tile(n), tile(n), over_halves(c_copy[:, c_slot(n), :]),
                                   ALU.mult).then_inc(output_pool, 1)

            def prepare(k, s, i):
                if k >= ITEMS:
                    return
                m = k % 2
                if s == AT_LOW:
                    wait(pool, mid_ready, k + 1, 1, i)
                    pool.tensor_tensor(split[m][0:32, :], split_rest[0:32, :], split[m][0:32, :],
                                       ALU.subtract).then_inc(split_ready, 1)
                if s == AT_LOG1P:
                    wait(pool, lost_ready, k + 1, 1, i)
                    wait(pool, ln_ready, k + 1, 1, i)
                    pool.tensor_tensor(sp_ln[:, :, :], sp_ln[:, :, :], sp_one[:, :, :],
                                       ALU.subtract).then_inc(log1p_ready, 1)

            pool.wait_ge(identities, 2 + PARTS)
            for part in range(PARTS - len(SPARES)):
                pool.memset(pad[part][:, :, :, :], 0.0).then_inc(pads_zero, 1)
            for s in range(NST):
                prepare(0, s, 0)
            for n in range(POOL_LEAD):
                times_b(n, 0)

            def slot(k, s, i):
                n = NST * k + s
                times_b(n + POOL_LEAD, i)
                times_c(n - 1, i)
                prepare(k + 1, s, i)

            run_items(pool, slot)
            times_c(LAST - 1, 0)
            for part in SPARE_PADS:
                pool.wait_ge(scanned, HALVES * (LAST - NST + max(SPARES) + 1))
                pool.memset(pad[part][:, :, :, :], 0.0).then_inc(pads_zero, 1)

        @block.scalar
        def _(act):
            def copy(o, i_):
                return act.activation(o, i_, ACT.Copy)

            load_x_tokens(act, 0, 1)
            for m in range(2):
                load_vectors(act, m)

            def a_log(m):
                act.wait_ge(load_w[m], W_LOADS)
                act.activation(a_neg[m][:, :, :], a_neg[m][:, :, :], ACT.Exp).then_inc(a_exp, 1)

            a_log(0)
            for g in range(0, FIRST, 2):
                setup_copy(act, copy, g, setup_act)

            def kernels(s):
                if s == AT_KERNELS[0] - 1:
                    act.wait_ge(load_k, K_LOADS)
                    for n in range(2):
                        act.activation(k_sign[n], k_raw[n], ACT.Sign).then_inc(k_signed, 1)
                if s in AT_KERNELS[:2]:
                    n = AT_KERNELS.index(s)
                    act.wait_ge(k_mm, n + 1)
                    copy(k_t[n][:, 0:8, :].rearrange("p a e -> p (a e)"), work[:, :].bitcast(BF16)).then_inc(k_copied, 1)

            def copy_b(n, i):
                if n >= LAST:
                    return
                wait(act, b_ready, n + 1, NST, i)
                wait(act, input_ready, n + 1 - B_COPIES, NST, i)
                copy(b_copy[:, n % B_COPIES, :], b_row[:, :]).then_inc(b_copied, 1)

            def copy_c(n, i):
                if n >= LAST or n % NST not in POOL_C:
                    return
                wait(act, c_ready, n + 1, NST, i)
                wait(act, output_pool, taken(POOL_C, n) + 1 - C_COPIES, len(POOL_C), i)
                copy(c_copy[:, c_slot(n), :], c_row[:, :]).then_inc(c_copied, 1)

            def decays(n, i):
                if n >= LAST:
                    return
                m, s = n // NST % 2, n % NST
                wait(act, dt_ready, n // NST + 1, 1, i)
                for h in range(HALVES):
                    wait(act, scanned, decay_free(n, h), 2 * NST, i)
                    act.activation(decay_place(n, h).rearrange("p (q l) -> p q l", l=L)[:, :, 1:],
                                   dt[m][:, h, :].rearrange("p (q l) -> p q l", l=L)[:, :, 1:],
                                   ACT.Exp, scale=a_neg[m][:, h, s:s + 1]).then_inc(decay_ready, 1)

            def prepare(k, s, i):
                if k >= ITEMS:
                    return
                m = k % 2
                mm = 7 * k
                if s == AT_SILU:
                    wait(act, cv_ready, 2 * k + 2, 2, i)
                    act.activation(xc[m][:, :, :], cv[:, :, :], ACT.Silu).then_inc(xc_ready, 1)
                    wait(act, z_ready, 2 * k + 2, 2, i)
                    act.activation(gate[m][:, :, :], gate[m][:, :, :], ACT.Silu).then_inc(gate_ready, 1)
                    act.preload_act_table_set("natural_log_exp_and_others")
                if s == AT_DBC:
                    wait(act, pre_mm, mm + 5, 7, i)
                    wait(act, rest_ready, k, 1, i)
                    copy(dbc[:, :], work[0:PARTS * 32 + RANK, :]).then_inc(dbc_ready, 1)
                if s == AT_HIGH:
                    wait(act, dbc_ready, k + 1, 1, i)
                    wait(act, c_ready, NST * (k - 1), NST, i)
                    copy(split[m][:, :], dbc[0:PARTS * 32, :]).then_inc(hi_ready, 1)
                if s == AT_MID:
                    wait(act, rest_ready, k + 1, 1, i)
                    copy(split[m][0:64, :], split_rest[:, :]).then_inc(mid_ready, 1)
                if s in (AT_DT, AT_DT + 1):
                    h = s - AT_DT
                    wait(act, pre_mm, mm + 5 + h + 1, 7, i)
                    if h == 0:
                        wait(act, dt_ready, k, 1, i)
                    act.activation(sp_e[:, h, :], work[:, :], ACT.Abs, bias=b_dt[m][:, h:h + 1]).then_inc(abs_ready, 1)
                    wait(act, decay_ready, 2 * NST * (k - 1), 2 * NST, i)
                    act.activation(dt[m][:, h, :], work[:, :], ACT.Relu,
                                   bias=b_dt[m][:, h:h + 1]).then_inc(relu_ready, 1)
                if s == AT_EXP:
                    wait(act, abs_ready, 2 * k + 2, 2, i)
                    act.activation(sp_e[:, :, :], sp_e[:, :, :], ACT.Exp, scale=-1.0).then_inc(exp_ready, 1)
                if s == AT_LN:
                    wait(act, exp_ready, k + 1, 1, i)
                    act.activation(sp_one[:, :, :], sp_e[:, :, :], ACT.Identity, bias=1.0).then_inc(one_ready, 1)
                    act.activation(sp_ln[:, :, :], sp_e[:, :, :], ACT.Ln, bias=1.0).then_inc(ln_ready, 1)

            def copy_z(k, s, i):
                if k < ITEMS and s in (AT_Z, AT_Z + 1):
                    m, h = k % 2, s - AT_Z
                    wait(act, pre_mm, 7 * k + 2 + h + 1, 7, i)
                    wait(act, gated, k - 1, 1, i)
                    copy(gate[m][:, h, :], work[:, :]).then_inc(z_ready, 1)

            def copy_projected(k, h, i):
                if k >= ITEMS:
                    return
                wait(act, pre_mm, 7 * k + h + 1, 7, i)
                wait(act, xc_ready, k, 1, i)
                act.activation(cv[:, h, :], work[:, :], ACT.Identity,
                               bias=conv_b[k % 2][:, h:h + 1]).then_inc(cv_ready, 1)

            act.wait_ge(setup_dve, FIRST // 2)
            for h in range(HALVES):
                copy_projected(0, h, 0)
            for s in range(NST):
                copy_z(0, s, 0)
                prepare(0, s, 0)
                if s == 0:
                    a_log(1)
                if s % 2 == 0 and FIRST + s < NG:
                    setup_copy(act, copy, FIRST + s, setup_act)
                if 0 <= s - AT_EARLY < LEAD:
                    copy_b(s - AT_EARLY, 0)
                if s == AT_U + 1:
                    act.wait_ge(a_ready, 2)
                    act.wait_ge(zeros, 4 + len(SPARES) + DECAYS)
                    decays(0, 0)
                if s in AT_X_FIRST:
                    act.wait_ge(setup_dve, (FIRST + 5) // 2 + 1)
                    copy_projected(1, AT_X_FIRST.index(s), 0)
            act.wait_ge(setup_dve, NG // 2)

            def slot(k, s, i):
                n = NST * k + s
                if s + 1 in SPARES:
                    decays(n + 2, i)
                elif s not in SPARES:
                    decays(n + 1, i)
                if s != AT_SILU + 1:
                    copy_b(n + LEAD, i)
                copy_c(n, i)
                if s == AT_SILU:
                    for spare_step in SPARES:
                        decays(NST * k + spare_step, i)
                copy_z(k + 1, s, i)
                if s == AT_SILU:
                    copy_b(n + LEAD + 1, i)
                prepare(k + 1, s, i)
                if k == 0:
                    kernels(s)
                for item, h in due(k, s, AT_X, AT_X_OUT):
                    copy_projected(item + 2, h, i)

            run_items(act, slot)

            for layer in range(2):
                act.wait_ge(bn_mv, layer + 1)
                if layer == 0:
                    act.activation(bn_tmp[:, 0:1], mv[:, 1:2], ACT.Sqrt, bias=eps[:, 0:1]).then_inc(bn_std, 1)
                else:
                    act.activation(bn_tmp[:, 0:1], mv[:, 1:2], ACT.Sqrt, bias=eps[:, 0:1],
                                   scale=k_mean_sq[:, 0:1]).then_inc(bn_std, 1)
                act.wait_ge(bn_ready, layer + 1)

                def normalized(n, target, three_d):
                    src = res[:, n // 2, n % 2 * CHUNK:(n % 2 + 1) * CHUNK] if layer == 0 else bank[n][:, :]
                    if three_d:
                        src = src.rearrange("p (r w) -> p r w", w=W)
                    return act.activation(target, src, ACT.Relu, bias=bn_b[layer][:, 0:1],
                                          scale=bn_a[layer][:, 0:1])

                if layer == 0:
                    act.wait_ge(pads_zero, PARTS)
                for first in range(0, TILES, 2):
                    for n in (first, first + 1):
                        normalized(n, inner(0, n), True).then_inc(act_hi, 1)
                    for n in (first, first + 1):
                        g = TILES * layer + n
                        if g >= 2:
                            act.wait_ge(act_rest, g - 1)
                        normalized(n, act_f[:, n % 2, :], False).then_inc(act_full, 1)

        @block.vector
        def _(dve):
            for m in range(2):
                dve.memset(w_dt_raw[m][:, :, 0:PARTS * 32], 0.0).then_inc(zeros, 1)
            dve.memset(x_t[:, :, 0:LPAD], 0.0).then_inc(zeros, 1)
            for h in range(DECAYS):
                dve.memset(decay[h][:, :].rearrange("p (q l) -> p q l", l=L)[:, :, 0:1], 0.0).then_inc(zeros, 1)
            for decays in spare:
                dve.memset(decays.rearrange("p h (q l) -> p (h q) l", l=L)[:, :, 0:1], 0.0).then_inc(zeros, 1)
            dve.memset(eps[:, :], EPS).then_inc(zeros, 1)

            def scale_taps(m):
                dve.wait_ge(load_w[m], W_LOADS)
                for h in range(HALVES):
                    dve.tensor_tensor(w_tap_raw[m][:, h, :, :],
                                      w_in_raw[m][:, h, :].unsqueeze(1).to_broadcast([128, KCONV, 128]),
                                      conv_w[m][:, h, :].unsqueeze(2).to_broadcast([128, KCONV, 128]),
                                      ALU.mult).then_inc(taps_ready, 1)

            def negate(m):
                dve.wait_ge(a_exp, m + 1)
                dve.tensor_scalar(a_neg[m][:, :, :], a_neg[m][:, :, :], -1.0, None, ALU.mult).then_inc(a_ready, 1)

            scale_taps(0)
            negate(0)
            for g in range(1, FIRST, 2):
                setup_copy(dve, dve.tensor_copy, g, setup_dve)
            scale_taps(1)

            def kernels(s):
                if s == AT_KERNELS[0]:
                    dve.wait_ge(load_k, K_LOADS)
                if s in AT_KERNELS[:2]:
                    n = AT_KERNELS.index(s)
                    dve.tensor_reduce(k_abs[:, n:n + 1], k_raw[n], AX.X, ALU.add,
                                      apply_absolute_value=True).then_inc(k_summed, 1)
                if s == AT_KERNELS[2]:
                    dve.wait_ge(k_mm, 3)
                    for n in range(2):
                        dve.tensor_copy(k_t[n][:, 8, :],
                                        work[:, 64 * n:64 * n + 64].bitcast(BF16)).then_inc(k_copied, 1)
                    dve.tensor_scalar(k_mean[:, :], work[:, 256:258], 1.0 / WCOUNT, None,
                                      ALU.mult).then_inc(k_mean_ready, 1)
                    dve.wait_ge(k_mean_ready, 1)
                    dve.tensor_tensor(k_mean_sq[:, :], k_mean[:, :], k_mean[:, :], ALU.mult).then_inc(k_mean_ready, 1)

            def scan(n, i):
                wait(dve, input_ready, n + 1, NST, i)
                for h in range(HALVES):
                    wait(dve, decay_ready, 2 * n + h + 1, 2 * NST, i)
                    dve.tensor_tensor_scan(tile(n)[:, h, :], decay_place(n, h), tile(n)[:, h, :], 0.0,
                                           ALU.mult, ALU.add).then_inc(scanned, 1)

            def times_c(n, i):
                if n < 0 or n % NST in POOL_C:
                    return
                wait(dve, scanned, 2 * n + 2, 2 * NST, i)
                wait(dve, c_ready, n + 1, NST, i)
                dve.tensor_tensor(tile(n), tile(n), over_halves(c_row[:, :]), ALU.mult).then_inc(output_dve, 1)

            def prepare(k, s, i):
                if k >= ITEMS:
                    return
                m = k % 2
                if s == AT_REST:
                    wait(dve, hi_ready, k + 1, 1, i)
                    wait(dve, split_ready, k, 1, i)
                    dve.tensor_tensor(split_rest[:, :], dbc[0:64, :], split[m][0:64, :],
                                      ALU.subtract).then_inc(rest_ready, 1)
                if s == AT_LOST:
                    wait(dve, one_ready, k + 1, 1, i)
                    dve.scalar_tensor_tensor(sp_one[:, :, :], sp_one[:, :, :], 1.0, sp_e[:, :, :],
                                             ALU.subtract, ALU.subtract).then_inc(lost_ready, 1)
                if s == AT_U:
                    wait(dve, log1p_ready, k + 1, 1, i)
                    wait(dve, relu_ready, 2 * k + 2, 2, i)
                    dve.tensor_tensor(dt[m][:, :, :], sp_ln[:, :, :], dt[m][:, :, :], ALU.add).then_inc(dt_ready, 1)
                    wait(dve, dt_ready, k + 1, 1, i)
                    wait(dve, xc_ready, k + 1, 1, i)
                    wait(dve, scanned, 2 * NST * (k - 1), 2 * NST, i)
                    dve.tensor_tensor(u[m][:, :, :], dt[m][:, :, :], xc[m][:, :, :], ALU.mult).then_inc(u_ready, 1)

            def post(k, i):
                m, j = k % 2, k // 2 % 2
                wait(dve, summed, NST * (k + 1), NST, i)
                for h in range(HALVES):
                    dve.scalar_tensor_tensor(xc[m][:, h, :], xc[m][:, h, :], d_skip[m][:, h:h + 1],
                                             y_sum[h][:, :], ALU.mult, ALU.add).then_inc(y_read, 1)
                wait(dve, y_read, 2 * k + 2, 2, i)
                wait(dve, gate_ready, k + 1, 1, i)
                dve.tensor_tensor(y_gated[:, 2 * m:2 * m + 2, j * CHUNK:(j + 1) * CHUNK], xc[m][:, :, :],
                                  gate[m][:, :, :], ALU.mult).then_inc(gated, 1)

            def add_output(k, part, i):
                b = k // ITEMS_PER_IMAGE - 1 + i
                wait_image(dve, out_mm, 2 * (k // ITEMS_PER_IMAGE - 1) + part + 1, i)
                dst = res[:, bass.ds(b, 1), part * CHUNK:(part + 1) * CHUNK].rearrange("p b n -> p (b n)")
                dve.tensor_tensor(dst, dst, projected(k, part)[:, :], ALU.add).then_inc(res_added, 1)

            for s in range(NST):
                prepare(0, s, 0)
                if s == 0:
                    negate(1)
                if s % 2 == 1 and FIRST + s < NG:
                    setup_copy(dve, dve.tensor_copy, FIRST + s, setup_dve)

            def slot(k, s, i):
                n = NST * k + s
                scan(n, i)
                times_c(n - 1, i)
                if s == AT_POST and k > 0:
                    post(k - 1, i)
                if out_half(k, s, 1, 2):
                    add_output(k, out_half(k, s, 1, 2)[0], i)
                prepare(k + 1, s, i)
                if k == ITEMS - 1 and 0 <= s - AT_STATS < TILES - 2:
                    statistics(0, s - AT_STATS)
                if k == 0:
                    kernels(s)
                    if s == NST - 1:
                        dve.wait_ge(k_copied, 4)
                        dve.wait_ge(load_res, 16 * NB)

            def statistics(layer, n):
                if layer == 0:
                    dve.wait_ge(res_added, n // 2 * 2 + 2)
                    src = res[:, n // 2, n % 2 * CHUNK:(n % 2 + 1) * CHUNK]
                else:
                    dve.wait_ge(conv_mm, n + 1)
                    src = bank[n][:, :]
                dve.bn_stats(stats[:, n, :], src).then_inc(stat_done, 1)

            run_items(dve, slot)
            times_c(LAST - 1, 0)
            post(ITEMS - 1, 0)
            for part in range(2):
                add_output(ITEMS, part, 0)

            for layer in range(2):
                for n in range(TILES - 2 if layer == 0 else 0, TILES):
                    statistics(layer, n)
                dve.wait_ge(stat_done, TILES * (layer + 1))
                dve.bn_aggr(mv[:, :], stats[:, :, :].rearrange("p a b -> p (a b)")).then_inc(bn_mv, 1)
                dve.wait_ge(bn_std, layer + 1)
                q = 3 * layer
                dve.reciprocal(bn_tmp[:, 1:2], bn_tmp[:, 0:1]).then_inc(bn_step, 1)
                dve.wait_ge(bn_step, q + 1)
                if layer == 0:
                    dve.tensor_tensor(bn_a[0][:, :], bn_tmp[:, 1:2], gamma[0][:, :], ALU.mult).then_inc(bn_step, 1)
                else:
                    dve.scalar_tensor_tensor(bn_a[1][:, :], bn_tmp[:, 1:2], k_mean[:, 0:1], gamma[1][:, :],
                                             ALU.mult, ALU.mult).then_inc(bn_step, 1)
                dve.wait_ge(bn_step, q + 2)
                dve.wait_ge(bn_mv, layer + 1)
                dve.tensor_tensor(bn_tmp[:, 2:3], mv[:, 0:1], bn_a[layer][:, :], ALU.mult).then_inc(bn_step, 1)
                dve.wait_ge(bn_step, q + 3)
                dve.tensor_tensor(bn_b[layer][:, :], beta[layer][:, :], bn_tmp[:, 2:3],
                                  ALU.subtract).then_inc(bn_ready, 1)
                for n in range(TILES):
                    g = TILES * layer + n
                    rest = act_r[:, n % 2, :].rearrange("p (r w) -> p r w", w=W)
                    full = act_f[:, n % 2, :].rearrange("p (r w) -> p r w", w=W)
                    dve.wait_ge(act_full, g + 1)
                    dve.wait_ge(act_hi, g + 1)
                    if g >= 2:
                        dve.wait_ge(act_lo, g - 1)
                    dve.tensor_tensor(rest, full, inner(0, n), ALU.subtract).then_inc(act_rest, 1)
                    dve.wait_ge(act_rest, g + 1)
                    dve.tensor_copy(inner(1, n), rest).then_inc(act_mid, 1)
                    dve.wait_ge(act_mid, g + 1)
                    dve.tensor_tensor(inner(2, n), rest, inner(1, n), ALU.subtract).then_inc(act_lo, 1)
            for n in range(TILES):
                b, half = n // 2, n % 2
                dst = res[:, b, half * CHUNK:(half + 1) * CHUNK]
                dve.wait_ge(conv_mm, TILES + n + 1)
                dve.scalar_tensor_tensor(dst, bank[n][:, :], k_mean[:, 1:2], dst,
                                         ALU.mult, ALU.add).then_inc(y_ready, 1)

        @block.tensor
        def _(pe):
            def transposes(g):
                what, which, sources, cols, _, _ = GROUPS[g]
                last = g - SETUP_BANKS
                if last >= 0:
                    pe.wait_ge(setup_act if last % 2 == 0 else setup_dve, last // 2 + 1)
                if what == "x":
                    pe.wait_ge(load_x, 16 * X_LOADS[which])
                else:
                    pe.wait_ge(load_w[which], W_LOADS)
                    pe.wait_ge(taps_ready, HALVES * (which + 1))
                for j, src in enumerate(sources):
                    rows = src.shape[0]
                    mm = pe.transpose(setup_bank(g)[0:src.shape[1], cols * j:cols * j + rows], src,
                                      ident[0:rows, 0:rows])
                mm.then_inc(setup_mm, 1)

            def kernels(s):
                if s == AT_KERNELS[0]:
                    pe.wait_ge(relu_ready, 2 * 2)
                    pe.wait_ge(k_signed, 2)
                if s in AT_KERNELS[1:]:
                    pe.wait_ge(k_copied, s - AT_KERNELS[0])
                if s in AT_KERNELS[:2]:
                    taps = k_sign[AT_KERNELS.index(s)].rearrange("p (i q) -> p q i", q=TAPS)
                    for q in range(8):
                        mm = pe.transpose(work[:, 64 * q:64 * q + 64].bitcast(BF16), taps[:, q, :], ident16[:, :])
                    mm.then_inc(k_mm, 1)
                if s == AT_KERNELS[2]:
                    for n in range(2):
                        taps = k_sign[n].rearrange("p (i q) -> p q i", q=TAPS)
                        pe.transpose(work[:, 64 * n:64 * n + 64].bitcast(BF16), taps[:, 8, :], ident16[:, :])
                    pe.wait_ge(k_summed, 2)
                    pe.matmul(work[:, 256:258], ones[:, :], k_abs[:, :]).then_inc(k_mm, 1)
                if s == AT_KERNELS[2] + 1:
                    pe.wait_ge(k_mean_ready, 1)

            pe.wait_ge(identities, 2)
            pe.wait_ge(zeros, 3)
            for g in range(FIRST):
                transposes(g)

            def spread(row, n, ready, i):
                wait(pe, split_ready, n // NST + 1, 1, i)
                target = b_row if row < NST else c_row
                pe.matmul(target[:, :], sel[:, row, :], split[n // NST % 2][:, :]).then_inc(ready, 1)

            def spread_b(n, i):
                if n >= LAST:
                    return
                wait(pe, b_copied, n, NST, i)
                spread(n % NST, n, b_ready, i)

            def spread_c(n, i):
                if (n - 1) % NST in POOL_C:
                    wait(pe, c_copied, taken(POOL_C, n), len(POOL_C), i)
                elif n > 0:
                    wait(pe, output_dve, n - taken(POOL_C, n), NST - len(POOL_C), i)
                spread(NST + n % NST, n, c_ready, i)

            def sum_states(n, i):
                if n < 0:
                    return
                wait_output(pe, n, i)
                if n % NST == 0:
                    wait(pe, y_read, 2 * (n // NST), 2, i)
                for h in range(HALVES):
                    mm = pe.matmul(y_sum[h][:, :], ident[:, :], tile(n)[:, h, :],
                                   start=(n % NST == 0), stop=(n % NST == NST - 1))
                mm.then_inc(summed, 1)

            def prepare(k, s, i):
                if k >= ITEMS:
                    return
                m = k % 2
                if s in (AT_GATE, AT_GATE + 1):
                    h = s - AT_GATE
                    if h == 0:
                        wait(pe, cv_ready, 2 * k + 2, 2, i)
                    else:
                        wait(pe, z_ready, 2 * k + 1, 2, i)
                    pe.matmul(by_sequence(work), w_z[m][:, h, :], chunk_of(k, LPAD, i)).then_inc(pre_mm, 1)
                if s == AT_DBC:
                    wait(pe, z_ready, 2 * k + 2, 2, i)
                    wait(pe, xc_ready, k + 1, 1, i)
                    for h in range(HALVES):
                        mm = pe.matmul(work[0:PARTS * 32 + RANK, :], w_x[m][:, h, :], xc[m][:, h, :],
                                       start=(h == 0), stop=(h == HALVES - 1))
                    mm.then_inc(pre_mm, 1)
                if s in (AT_DT, AT_DT + 1):
                    h = s - AT_DT
                    if h == 0:
                        wait(pe, dbc_ready, k + 1, 1, i)
                    else:
                        wait(pe, relu_ready, 2 * k + 1, 2, i)
                    pe.matmul(work[:, :], w_dt[m][PARTS * 32:, 128 * h:128 * h + 128],
                              dbc[PARTS * 32:, :]).then_inc(pre_mm, 1)

            def by_sequence(psum):
                return psum[:, :].rearrange("p (q l) -> p q l", l=L)

            def chunk_of(k, first, i):
                return x_t[:, bass.ds(k // 2 * CSEQ + i * (2 * CSEQ), CSEQ), first:first + L]

            def project(k, part, i):
                if k >= ITEMS:
                    return
                h, tap = part // KCONV, part % KCONV
                if part == 0:
                    wait(pe, relu_ready, 2 * k, 2, i)
                if part == KCONV:
                    wait(pe, cv_ready, 2 * k + 1, 2, i)
                mm = pe.matmul(by_sequence(work), w_tap[k % 2][:, h, tap, :], chunk_of(k, tap, i),
                               start=(tap == 0), stop=(tap == KCONV - 1))
                if tap == KCONV - 1:
                    mm.then_inc(pre_mm, 1)

            def project_out(k, r, i):
                q = r % 4
                if r == 0:
                    wait(pe, gated, k // ITEMS_PER_IMAGE * ITEMS_PER_IMAGE, 1, i)
                    if k < ITEMS:
                        wait(pe, relu_ready, 2 * (k + 1) + 2, 2, i)
                if r == 4:
                    if k < ITEMS:
                        wait(pe, cv_ready, 2 * (k + 1) + 2, 2, i)
                        wait_image(pe, res_added, 2 * (k // ITEMS_PER_IMAGE) - 1, i)
                    else:
                        pe.wait_ge(b_copied, LAST)
                for g in range(4):
                    mm = pe.matmul(projected(k, r // 4)[:, 128 * q:128 * q + 128],
                                   y_gated[:, g, r:HW:8], w_out[g // 2][:, g % 2, :],
                                   start=(g == 0), stop=(g == 3), skip_group_check=True)
                if q == 3:
                    mm.then_inc(out_mm, 1)

            pe.wait_ge(setup_act, FIRST // 2)
            pe.wait_ge(setup_dve, FIRST // 2)
            for part in range(HALVES * KCONV):
                project(0, part, 0)
            for s in range(NST):
                prepare(0, s, 0)
                if FIRST + s < NG:
                    transposes(FIRST + s)
                if s == AT_EARLY:
                    pe.wait_ge(identities, 2 + PARTS)
                    pe.wait_ge(consts, 4)
                    pe.wait_ge(setup_act, FIRST // 2 + 1)
                    pe.wait_ge(setup_dve, FIRST // 2 + 1)
                if 0 <= s - AT_EARLY < LEAD:
                    spread_b(s - AT_EARLY, 0)
                for part in range(HALVES * KCONV):
                    if AT_PROJ_FIRST[part] == s:
                        project(1, part, 0)
            pe.wait_ge(setup_act, NG // 2)
            pe.wait_ge(setup_dve, NG // 2)

            def slot(k, s, i):
                n = NST * k + s
                spread_b(n + LEAD, i)
                if LAG < s <= CATCH_UP:
                    sum_states(n - LAG - 1, i)
                if s < LAG or s >= CATCH_UP:
                    sum_states(n - LAG, i)
                spread_c(n, i)
                if out_half(k, s, 1, 3):
                    wait_image(pe, res_added, 2 * (k // ITEMS_PER_IMAGE) - 1 + out_half(k, s, 1, 3)[0], i)
                prepare(k + 1, s, i)
                if out_half(k, s, 2):
                    half, j = out_half(k, s, 2)
                    project_out(k, 4 * half + 2 * j, i)
                    project_out(k, 4 * half + 2 * j + 1, i)
                if k == 0:
                    kernels(s)
                for item, part in due(k, s, AT_PROJ, AT_PROJ_OUT):
                    project(item + 2, part, i)

            run_items(pe, slot)
            for n in range(LAST - LAG, LAST):
                sum_states(n, 0)
            for r in range(8):
                project_out(ITEMS, r, 0)

            for layer in range(2):
                for n in range(TILES):
                    b, r = n // 2, ROWS * (n % 2)
                    for part in range(PARTS):
                        if n % 2 == 0:
                            pe.wait_ge((act_hi, act_mid, act_lo)[part], TILES * layer + n + 2)
                            if layer == 1 and part == 0:
                                pe.wait_ge(act_full, TILES + n + 2)
                        for q in range(TAPS):
                            src = pad[part][:, b, r + q // 3:r + q // 3 + ROWS, q % 3:q % 3 + W]
                            mm = pe.matmul(bank[n][:, :].rearrange("p (r w) -> p r w", w=W), k_t[layer][:, q, :], src,
                                           start=(q == 0 and part == 0), stop=(q == TAPS - 1 and part == PARTS - 1))
                    mm.then_inc(conv_mm, 1)


_INS = ['x'] + [f'L0_conv_{n}{m}' for m in (1, 2) for n in
                ('W_in', 'conv_w', 'conv_b', 'W_x', 'W_dt', 'b_dt', 'A_log', 'D_skip', 'W_out')] + \
       [f'L1_conv_{n}' for n in ('gamma0', 'beta0', 'w0', 'gamma1', 'beta1', 'w1')]


def kernel(**inputs):
    import numpy as _np
    import concourse.bacc as _bacc
    from concourse import mybir as _mybir
    from concourse.bass_utils import run_bass_kernel_spmd as _run

    nc = _bacc.Bacc("TRN2", target_bir_lowering=False, num_devices=1)
    arrays, tensors = {}, {}
    for name in _INS:
        a = _np.ascontiguousarray(inputs[name])
        arrays[f"in_{name}_dram"] = a
        tensors[name] = nc.dram_tensor(f"in_{name}_dram", a.shape, _mybir.dt.from_np(a.dtype),
                                       kind="ExternalInput").ap()
    out = nc.dram_tensor("out_0_dram", (NB, C, H, W), F32, kind="ExternalOutput").ap()
    mamba_conv_kernel(nc, tensors, out)
    r = _run(nc, [arrays], core_ids=[0])
    return r.results[0]["out_0_dram"]
```
